# Optimizing a Trainium2 kernel written in Bass

```python
import numpy as np
import jax
import jax.numpy as jnp

def _softmax(x, axis=-1):
    return jax.nn.softmax(x, axis=axis)

def _gelu(x):
    return jax.nn.gelu(x, approximate=True)

def _silu(x):
    return jax.nn.silu(x)

def _sigmoid(x):
    return jax.nn.sigmoid(x)

def _layernorm(x, axis=-1, eps=1e-05):
    m = jnp.mean(x, axis=axis, keepdims=True)
    v = jnp.var(x, axis=axis, keepdims=True)
    return (x - m) / jnp.sqrt(v + eps)

def _scatter_add(tgt, idx, src, axis=0):
    return tgt.at[idx].add(src)

def _segment_sum(src, seg, n):
    return jax.ops.segment_sum(src, seg, n)
kernel_name = 'mk_seq_preln_d1_jaxref_r4_f11473'

def setup_inputs(seed: int=0):
    np.random.seed(seed)
    _w = jnp.asarray

    def _L0_attn_setup():
        import jax, jax.numpy as jnp
        import numpy as np
        D = 256
        H = 16
        HKV = 4
        HD = D // H
        L = 64
        EPS = 1e-06
        LN_EPS = 1e-05
        B, S = (2, 256)

        def _feat(x):
            return jax.nn.elu(x) + 1.0
        key = jax.random.key(seed)
        ks = jax.random.split(key, 8)
        w = lambda k, shape: jax.random.normal(k, shape, jnp.float32) * 0.02
        return {'x': jax.random.normal(ks[0], (B, S, D), jnp.float32), 'Wq': w(ks[1], (D, D)), 'bq': jnp.zeros((D,), jnp.float32), 'Wk': w(ks[2], (D, HKV * HD)), 'bk': jnp.zeros((HKV * HD,), jnp.float32), 'Wv': w(ks[3], (D, HKV * HD)), 'bv': jnp.zeros((HKV * HD,), jnp.float32), 'Wc': w(ks[4], (HKV * HD, L)), 'We': w(ks[5], (L, HKV * HD)), 'Wo': w(ks[6], (D, D)), 'bo': jnp.zeros((D,), jnp.float32), 'gamma': jnp.ones((D,), jnp.float32), 'beta': jnp.zeros((D,), jnp.float32)}
    _L0_attn_in = _L0_attn_setup()

    def _L0_ffn_setup():
        import jax, jax.numpy as jnp
        import numpy as np
        DIM = 256

        def _reference_tuple_inner(x, W_r, W_k, W_v, mu_r, mu_k):
            B, T, C = x.shape
            x_prev = jnp.concatenate([jnp.zeros((B, 1, C), x.dtype), x[:, :-1, :]], axis=1)
            xr = mu_r * x + (1.0 - mu_r) * x_prev
            xk = mu_k * x + (1.0 - mu_k) * x_prev
            r = jax.nn.sigmoid(jnp.einsum('btc,dc->btd', xr, W_r))
            k = jnp.einsum('btc,dc->btd', xk, W_k)
            k_act = jnp.square(jax.nn.relu(k))
            out = r * jnp.einsum('btc,dc->btd', k_act, W_v)
            new_state = x[:, -1, :]
            return (out, new_state)
        key = jax.random.key(seed)
        ks = jax.random.split(key, 6)
        B, T, C = (8, 512, DIM)
        x = jax.random.normal(ks[0], (B, T, C), dtype=jnp.float32)
        s = 1.0 / np.sqrt(C)
        W_r = jax.random.uniform(ks[1], (C, C), jnp.float32, -s, s)
        W_k = jax.random.uniform(ks[2], (C, C), jnp.float32, -s, s)
        W_v = jax.random.uniform(ks[3], (C, C), jnp.float32, -s, s)
        mu_r = jax.random.uniform(ks[4], (C,), jnp.float32)
        mu_k = jax.random.uniform(ks[5], (C,), jnp.float32)
        return {'x': x, 'W_r': W_r, 'W_k': W_k, 'W_v': W_v, 'mu_r': mu_r, 'mu_k': mu_k}
    _L0_ffn_in = _L0_ffn_setup()
    _d = {'L0_attn_x': _L0_attn_in['x'], 'L0_attn_Wq': _L0_attn_in['Wq'], 'L0_attn_bq': _L0_attn_in['bq'], 'L0_attn_Wk': _L0_attn_in['Wk'], 'L0_attn_bk': _L0_attn_in['bk'], 'L0_attn_Wv': _L0_attn_in['Wv'], 'L0_attn_bv': _L0_attn_in['bv'], 'L0_attn_Wc': _L0_attn_in['Wc'], 'L0_attn_We': _L0_attn_in['We'], 'L0_attn_Wo': _L0_attn_in['Wo'], 'L0_attn_bo': _L0_attn_in['bo'], 'L0_attn_gamma': _L0_attn_in['gamma'], 'L0_attn_beta': _L0_attn_in['beta'], 'L0_ffn_W_r': _L0_ffn_in['W_r'], 'L0_ffn_W_k': _L0_ffn_in['W_k'], 'L0_ffn_W_v': _L0_ffn_in['W_v'], 'L0_ffn_mu_r': _L0_ffn_in['mu_r'], 'L0_ffn_mu_k': _L0_ffn_in['mu_k']}
    _x0 = _d['L0_attn_x']
    _d['L0_attn_x'] = jax.random.normal(jax.random.fold_in(jax.random.key(seed), 1), (4, 1024, 256), dtype=_x0.dtype)
    del _x0
    return _d

def reference(L0_attn_x, L0_attn_Wq, L0_attn_bq, L0_attn_Wk, L0_attn_bk, L0_attn_Wv, L0_attn_bv, L0_attn_Wc, L0_attn_We, L0_attn_Wo, L0_attn_bo, L0_attn_gamma, L0_attn_beta, L0_ffn_W_r, L0_ffn_W_k, L0_ffn_W_v, L0_ffn_mu_r, L0_ffn_mu_k):

    def _L0_attn_ref(x, Wq, bq, Wk, bk, Wv, bv, Wc, We, Wo, bo, gamma, beta):
        import jax, jax.numpy as jnp
        import numpy as np
        D = 256
        H = 16
        HKV = 4
        HD = D // H
        L = 64
        EPS = 1e-06
        LN_EPS = 1e-05
        B, S = (2, 256)

        def _feat(x):
            return jax.nn.elu(x) + 1.0
        b, s, _ = x.shape
        residual = x
        q = x @ Wq + bq
        k = x @ Wk + bk
        v = x @ Wv + bv
        k = k @ Wc @ We
        v = v @ Wc @ We
        q = q.reshape(b, s, H, HD).transpose(0, 2, 1, 3)
        k = k.reshape(b, s, HKV, HD).transpose(0, 2, 1, 3)
        v = v.reshape(b, s, HKV, HD).transpose(0, 2, 1, 3)
        rep = H // HKV
        k = jnp.repeat(k, rep, axis=1)
        v = jnp.repeat(v, rep, axis=1)
        qf = _feat(q)
        kf = _feat(k)
        kv = jnp.einsum('bhsf,bhsd->bhsfd', kf, v)
        kv_cum = jnp.cumsum(kv, axis=2)
        num = jnp.einsum('bhsf,bhsfd->bhsd', qf, kv_cum)
        den = jnp.einsum('bhsf,bhsf->bhs', qf, jnp.cumsum(kf, axis=2))[..., None] + EPS
        o = num / den
        o = o.transpose(0, 2, 1, 3).reshape(b, s, D)
        o = o @ Wo + bo
        y = residual + o
        mu = jnp.mean(y, axis=-1, keepdims=True)
        var = jnp.var(y, axis=-1, keepdims=True)
        return (y - mu) / jnp.sqrt(var + LN_EPS) * gamma + beta

    def _L0_ffn_ref(x, W_r, W_k, W_v, mu_r, mu_k):
        import jax, jax.numpy as jnp
        import numpy as np
        DIM = 256

        def _reference_tuple_inner(x, W_r, W_k, W_v, mu_r, mu_k):
            B, T, C = x.shape
            x_prev = jnp.concatenate([jnp.zeros((B, 1, C), x.dtype), x[:, :-1, :]], axis=1)
            xr = mu_r * x + (1.0 - mu_r) * x_prev
            xk = mu_k * x + (1.0 - mu_k) * x_prev
            r = jax.nn.sigmoid(jnp.einsum('btc,dc->btd', xr, W_r))
            k = jnp.einsum('btc,dc->btd', xk, W_k)
            k_act = jnp.square(jax.nn.relu(k))
            out = r * jnp.einsum('btc,dc->btd', k_act, W_v)
            new_state = x[:, -1, :]
            return (out, new_state)
        return _reference_tuple_inner(x, W_r, W_k, W_v, mu_r, mu_k)[0]
    x = L0_attn_x
    x = x + _L0_attn_ref(_layernorm(x, axis=-1), L0_attn_Wq, L0_attn_bq, L0_attn_Wk, L0_attn_bk, L0_attn_Wv, L0_attn_bv, L0_attn_Wc, L0_attn_We, L0_attn_Wo, L0_attn_bo, L0_attn_gamma, L0_attn_beta)
    x = x + _L0_ffn_ref(_layernorm(x, axis=-1), L0_ffn_W_r, L0_ffn_W_k, L0_ffn_W_v, L0_ffn_mu_r, L0_ffn_mu_k)
    return x

_drawn_inputs = setup_inputs


def setup_inputs(seed=0):
    import zlib

    import numpy as np

    out = dict(_drawn_inputs(seed))
    spreads = {'L0_attn_bq': (0.0, 2.0),
     'L0_attn_bk': (0.0, 2.0),
     'L0_attn_bv': (0.0, 0.8),
     'L0_attn_bo': (0.0, 0.522),
     'L0_attn_gamma': (1.0, 0.2),
     'L0_attn_beta': (0.0, 0.1)}
    factors = {'L0_attn_Wq': 8.0,
     'L0_attn_Wk': 8.0,
     'L0_attn_Wv': 8.0,
     'L0_attn_Wc': 8.0,
     'L0_attn_We': 8.0,
     'L0_attn_Wo': 8.0,
     'L0_ffn_W_r': 6.348,
     'L0_ffn_mu_r': 8.0}
    for name, (base, spread) in spreads.items():
        noise = np.random.default_rng([zlib.crc32(name.encode()), seed]).standard_normal(out[name].shape)
        drawn = base * np.exp(spread * noise) if base else spread * noise
        out[name] = jnp.asarray(drawn.astype(out[name].dtype))
    for name, factor in factors.items():
        out[name] = (out[name] * factor).astype(out[name].dtype)
    return out
```

```python
from contextlib import ExitStack

import concourse.bass as bass
from concourse import mybir

P = 128
ALU = mybir.AluOpType
ACT = mybir.ActivationFunctionType
F32 = mybir.dt.float32
AX_X = mybir.AxisListType.X

LN_EPS = 1e-5
DEN_EPS = 1e-6


def build(nc, x, wq, bq, wk, bk, wv, bv, wc, we, wo, bo, gamma, beta, w_r, w_k, w_v, mu_r, mu_k, out):
    NB, S, D = x.shape
    NC = S // P
    KD = D // P
    G, HD = 4, 16
    KV = G * HD
    HALF = P // 2
    T = NB * P
    assert D == 256 and NB == 4 and KV == wk.shape[1] and NC % 2 == 0

    def chunk_at(dram, start):
        return dram.rearrange("b t d -> b (t d)")[:, bass.ds(start, P * D)].rearrange("b (t d) -> t b d", d=D)

    with ExitStack() as ctx:
        def sb(name, *shape):
            return ctx.enter_context(nc.sbuf_tensor(name, [P, *shape], F32))

        def sem(name):
            return ctx.enter_context(nc.semaphore(name))

        def bank(name):
            return ctx.enter_context(nc.psum_tensor(name, [P, 512], F32))

        ps_x = [bank("ps_x0"), bank("ps_x1")]
        ps_y = [bank("ps_y0"), bank("ps_y1")]
        ps_z = [bank("ps_z0"), bank("ps_z1")]
        ps_w = [bank("ps_w0"), bank("ps_w1")]

        ident = sb("ident", P)
        tri = sb("tri", P)
        causal = sb("causal", HALF)
        head_ones = sb("head_ones", 32)
        head_rep = sb("head_rep", 2 * NB, P)
        spread = sb("spread", 2, P)
        row_mask = sb("row_mask", 2)
        neg_half, ln_eps = sb("neg_half", NB), sb("ln_eps", NB)
        ones64, wait_carrier = sb("ones64", P), sb("wait_carrier", 1)

        wc_in, we_in, wk_in, wv_in = sb("wc_in", 64), sb("we_in", 64), sb("wk_in", KD, KV), sb("wv_in", KD, KV)
        bkv_col = sb("bkv_col", 2)
        ffn_in = [sb(f"ffn_in{i}", KD, D) for i in range(3)]
        wq_sb = sb("wq_sb", KD, 2, P)
        wo_sb = sb("wo_sb", 2, D)
        bq_col, neg_bq, bq_1 = sb("bq_col", 2), sb("neg_bq", 2), sb("bq_1", 2)
        gamma_bc, beta_bc, bo_bc = sb("gamma_bc", D), sb("beta_bc", D), sb("bo_bc", D)
        mu_r_col, mu_k_col = sb("mu_r_col", KD), sb("mu_k_col", KD)
        wcT, wkvT, cewe, bkv_lhs = sb("wcT", 64), sb("wkvT", 2, D), sb("cewe", KV), sb("bkv_lhs", 2, P)
        wkv_sb, bkv_bc = sb("wkv_sb", KD, 2 * KV), sb("bkv_bc", 2 * KV)
        wrT, wkT, wvT = sb("wrT", KD, D), sb("wkT", KD, D), sb("wvT", KD, D)

        x_in = sb("x_in", NB, D)
        a_tok = [sb(f"a_tok{i}", NB, D) for i in range(2)]
        xb_tok = [sb(f"xb_tok{i}", NB, D) for i in range(2)]
        stats0, mv0, rstd0 = sb("stats0", NB, 6), sb("mv0", NB, 2), sb("rstd0", NB)
        aT = sb("aT", KD, T)
        eq, qf = sb("eq", 2, T), sb("qf", 2, T)
        kb, ek = sb("kb", NB, KV), sb("ek", NB, KV)
        v_tok = sb("v_tok", NB, KV)
        v_pad = sb("v_pad", 2, NB, G, 2, HD)
        v_half = sb("v_half", NB, 2, KV)
        kf = sb("kf", NB * G, 2, HD)
        kfT = sb("kfT", 2, T)
        ksum, ksum_carry = sb("ksum", T), sb("ksum_carry", NB)
        prod = sb("prod", 2, T)
        denT, den, rden, rdenT, rden_bc = sb("denT", T), sb("den", NB, 16), sb("rden", NB, 16), sb("rdenT", T), sb("rden_bc", 2, T)
        dstate = sb("dstate", NB, 2, P)
        state = [sb(f"state{i}", NB, 2, P) for i in range(2)]
        probs = sb("probs", 2, 2, 512)
        oT = sb("oT", 2, NB, 2, HALF)
        y_tok, t_tok, x2_tok, z_tok = sb("y_tok", NB, D), sb("t_tok", NB, D), sb("x2_tok", NB, D), sb("z_tok", NB, D)
        stats1, mv1, rstd1 = sb("stats1", NB, 6), sb("mv1", NB, 2), sb("rstd1", NB)
        stats2, mv2, rstd2, nbias2 = sb("stats2", NB, 6), sb("mv2", NB, 2), sb("rstd2", NB), sb("nbias2", NB)
        zT = sb("zT", KD, NB, P + 1)
        dz, xr, xk = sb("dz", KD * NB, P), sb("xr", KD, NB, P), sb("xk", KD, NB, P)
        relu_k, k_act = sb("relu_k", 2, T), sb("k_act", 2, T)
        tanh_r, gated, out_tok = sb("tanh_r", 2, 512), sb("gated", 2, 512), sb("out_tok", NB, D)

        weights_in, x_loaded, out_stored = sem("weights_in"), sem("x_loaded"), sem("out_stored")
        pool_const, dve_const, prep_ps, prep_sb = sem("pool_const"), sem("dve_const"), sem("prep_ps"), sem("prep_sb")
        pool_link, bias_lhs = sem("pool_link"), sem("bias_lhs")
        s_st0, s_rs0, s_a, s_xb, s_ab = sem("stats0_done"), sem("rstd0_done"), sem("a_ready"), sem("xbeta_ready"), sem("abo_ready")
        s_aT_ps, s_aT = sem("aT_ps"), sem("aT_ready")
        s_q_ps, s_nq, s_eq, s_qf = sem("q_ps"), sem("negq"), sem("expq"), sem("qf_ready")
        s_kv_ps, s_kv, s_ek, s_ekm, s_kf = sem("kv_ps"), sem("kv_ready"), sem("expk"), sem("expk_min"), sem("kf_ready")
        s_kT_ps, s_kT, s_ks_ps, s_ks, s_carry = sem("kT_ps"), sem("kT_ready"), sem("ksum_ps"), sem("ksum_ready"), sem("carry_ready")
        s_dS_ps, s_dS, s_mid, s_next = sem("dstate_ps"), sem("dstate_ready"), sem("state_mid"), sem("state_next")
        s_prod, s_den_ps, s_denT, s_dtok_ps, s_den, s_rden = (
            sem("prod_ready"), sem("den_ps"), sem("denT_ready"), sem("dtok_ps"), sem("den_ready"), sem("rden_ready"))
        s_rT_ps, s_rT, s_rb_ps, s_rb = sem("rdenT_ps"), sem("rdenT_ready"), sem("rdenbc_ps"), sem("rdenbc_ready")
        s_sc, s_pr, s_o, s_oT = sem("scores_ps"), sem("probs_ready"), sem("o_ps"), sem("oT_ready")
        s_y_ps, s_y, s_st1, s_rs1, s_t, s_x2 = (
            sem("y_ps"), sem("y_ready"), sem("stats1_done"), sem("rstd1_done"), sem("t_ready"), sem("x2_ready"))
        s_st2, s_rs2, s_nb, s_z = sem("stats2_done"), sem("rstd2_done"), sem("nbias2_ready"), sem("z_ready")
        s_zT_ps, s_zcar, s_zT, s_dz, s_xk, s_xr = (
            sem("zT_ps"), sem("zshift_ready"), sem("zT_ready"), sem("dz_ready"), sem("xk_ready"), sem("xr_ready"))
        s_k_ps, s_rl, s_ka, s_r_ps, s_th, s_v_ps, s_gt, s_out = (
            sem("k_ps"), sem("relu_ready"), sem("kact_ready"), sem("r_ps"), sem("tanh_ready"), sem("v_ps"),
            sem("gated_ready"), sem("out_ready"))

        first = lambda c: isinstance(c, int) and c == 0

        def steps(eng, attention_and_mix, mix_only):
            attention_and_mix(0, 0, False, False)
            with eng.Fori(0, NC // 2 - 1) as pair:
                attention_and_mix(2 * pair + 1, 1, True, False)
                attention_and_mix(2 * pair + 2, 0, True, False)
            attention_and_mix(NC - 1, 1, True, True)
            mix_only(NC - 1, 1)

        block = ctx.enter_context(nc.Block())

        WEIGHT_DMAS = 0
        loads = [(wc_in[0:64, :], wc), (we_in[0:64, :], we),
                 (wk_in[:], wk.rearrange("(k p) n -> p k n", p=P)), (wv_in[:], wv.rearrange("(k p) n -> p k n", p=P)),
                 (bkv_col[0:64, 0:1], bk.rearrange("(n o) -> n o", o=1)),
                 (bkv_col[0:64, 1:2], bv.rearrange("(n o) -> n o", o=1))]
        for k in range(KD):
            for g in range(G):
                loads.append((wq_sb[:, k, :, 32 * g:32 * g + 32],
                              wq[k * P:(k + 1) * P, 64 * g:64 * g + 64].rearrange("p (a m) -> p a m", a=2)))
        for g in range(G):
            loads.append((bq_col[32 * g:32 * g + 32, :], bq[64 * g:64 * g + 64].rearrange("(a m) -> m a", a=2)))
        for w, dst in ((w_k, ffn_in[1]), (w_r, ffn_in[0]), (w_v, ffn_in[2])):
            loads.append((dst[:], w.rearrange("(k p) n -> p k n", p=P)))
        for g in range(G):
            loads.append((wo_sb[32 * g:32 * g + 32, :, :], wo[64 * g:64 * g + 64, :].rearrange("(a m) n -> m a n", a=2)))
        for v, dst in ((gamma, gamma_bc), (beta, beta_bc), (bo, bo_bc)):
            loads.append((dst[:], v.partition_broadcast(P)))
        for v, dst in ((mu_r, mu_r_col), (mu_k, mu_k_col)):
            loads.append((dst[:], v.rearrange("(k p) -> p k", p=P)))
        WEIGHT_DMAS = len(loads)

        @block.sync
        def _(sp):
            sp.sem_inc(out_stored, 16)
            sp.dma_start(x_in[:], chunk_at(x, 0)).then_inc(x_loaded, 16)
            with nc.allow_non_contiguous_dma(reason="bias and mixing vectors, one element a partition"):
                for dst, src in loads:
                    sp.dma_start(dst, src).then_inc(weights_in, 16)

            def attention_and_mix(c, p, mix, last):
                if not last:
                    sp.wait_ge(s_xb, c + 1)
                    sp.wait_ge(s_a, 4 * c + 4)
                    sp.dma_start(x_in[:], chunk_at(x, (c + 1) * P * D)).then_inc(x_loaded, 16)
                if mix:
                    store(c - 1)

            def store(m):
                sp.wait_ge(s_out, 2 * m + 3)
                sp.dma_start(chunk_at(out, m * P * D), out_tok[:]).then_inc(out_stored, 16)

            steps(sp, attention_and_mix, lambda m, p: store(m))
            sp.wait_ge(out_stored, 16 * NC + 16)

        @block.gpsimd
        def _(pool):
            links = [0]

            def link(ins):
                links[0] += 1
                ins.then_inc(pool_link, 1)
                pool.wait_ge(pool_link, links[0])

            link(nc.gpsimd.memset(ident[:], 0.0))
            link(nc.gpsimd.affine_select(out=ident[:], in_=ident[:], compare_op=ALU.not_equal, fill=1.0, base=0,
                                         pattern=[[-1, P]], channel_multiplier=1))
            link(nc.gpsimd.memset(tri[:], 1.0))
            link(nc.gpsimd.affine_select(out=tri[:], in_=tri[:], compare_op=ALU.is_ge, fill=0.0, base=0,
                                         pattern=[[1, P]], channel_multiplier=-1))
            link(nc.gpsimd.memset(causal[:], 1.0))
            for u in range(2):
                half = causal[HALF * u:HALF * u + HALF, :]
                link(nc.gpsimd.affine_select(out=half, in_=half, compare_op=ALU.is_ge, fill=0.0, base=0,
                                             pattern=[[1, HALF]], channel_multiplier=-1))
            link(nc.gpsimd.memset(head_ones[:], 1.0))
            link(nc.gpsimd.affine_select(out=head_ones[:], in_=head_ones[:], compare_op=ALU.is_ge, fill=0.0, base=0,
                                         pattern=[[-16, 32]], channel_multiplier=1))
            link(nc.gpsimd.affine_select(out=head_ones[:], in_=head_ones[:], compare_op=ALU.is_ge, fill=0.0, base=15,
                                         pattern=[[16, 32]], channel_multiplier=-1))
            link(nc.gpsimd.memset(head_rep[:], 1.0))
            rep = head_rep[:].rearrange("p r (n d) -> p r n d", d=HD)
            link(nc.gpsimd.affine_select(out=rep, in_=rep, compare_op=ALU.is_ge, fill=0.0, base=0,
                                         pattern=[[0, 2 * NB], [-16, 8], [0, HD]], channel_multiplier=1))
            link(nc.gpsimd.affine_select(out=rep, in_=rep, compare_op=ALU.is_ge, fill=0.0, base=15,
                                         pattern=[[0, 2 * NB], [16, 8], [0, HD]], channel_multiplier=-1))
            link(nc.gpsimd.memset(spread[:], 0.0))
            spr = spread[0:16, :, :].rearrange("p a (n d) -> p a n d", d=HD)
            link(nc.gpsimd.affine_select(out=spr, in_=spr, compare_op=ALU.not_equal, fill=1.0, base=0,
                                         pattern=[[-8, 2], [-1, 8], [0, HD]], channel_multiplier=1))
            link(nc.gpsimd.memset(ln_eps[:], LN_EPS))
            nc.gpsimd.memset(out_tok[:, 0, 0:1], 0.0).then_inc(s_out, 1)
            nc.gpsimd.memset(neg_half[:], -0.5).then_inc(pool_const, 1)
            pool.wait_ge(pool_const, 1)

            def rstd(dst, mv, eps, stats_done, stats_value, done, value):
                pool.wait_ge(stats_done, stats_value)
                nc.gpsimd.tensor_tensor(dst[:], mv[:, :, 1], eps[:], ALU.add).then_inc(done, 1)
                pool.wait_ge(done, value)
                nc.gpsimd.tensor_tensor(dst[:], dst[:], neg_half[:], ALU.pow).then_inc(done, 1)

            def norm_x(c, p):
                rstd(rstd0, mv0, ln_eps, s_st0, 8 * c + 8, s_rs0, 2 * c + 1)
                if not isinstance(c, int) or c >= 2:
                    pool.wait_ge(s_x2, 4 * c - 4)
                nc.gpsimd.tensor_tensor(xb_tok[p][:], x_in[:], beta_bc[:].unsqueeze(1).to_broadcast([P, NB, D]),
                                        ALU.add).then_inc(s_xb, 1)

            def add_bo(c, p):
                pool.wait_ge(s_aT_ps, 2 * c + 2)
                nc.gpsimd.tensor_tensor(a_tok[p][:], a_tok[p][:], bo_bc[:].unsqueeze(1).to_broadcast([P, NB, D]),
                                        ALU.add).then_inc(s_ab, 1)

            def mix_norms(m):
                rstd(rstd1, mv1, ln_eps, s_st1, 8 * m + 8, s_rs1, 2 * m + 1)
                rstd(rstd2, mv2, ln_eps, s_st2, 8 * m + 8, s_rs2, 2 * m + 1)

            def square_k(m):
                for i in range(2):
                    pool.wait_ge(s_rl, 2 * m + i + 1)
                    nc.gpsimd.tensor_tensor(k_act[:, i], relu_k[:, i], relu_k[:, i], ALU.mult).then_inc(s_ka, 1)

            def finish(m):
                pool.wait_ge(out_stored, 16 * m + 16)
                for i in range(2):
                    pool.wait_ge(s_gt, 2 * m + i + 2)
                    nc.gpsimd.tensor_tensor(out_tok[:, 2 * i:2 * i + 2, :],
                                            gated[:, i].rearrange("p (b d) -> p b d", b=2),
                                            x2_tok[:, 2 * i:2 * i + 2, :], ALU.add).then_inc(s_out, 1)

            def attention_and_mix(c, p, mix, last):
                pool.wait_ge(s_dS, c + 1)
                if not first(c):
                    pool.wait_ge(s_next, c)
                nc.gpsimd.tensor_tensor(state[p][:, :, 1, :], state[p][:, :, 0, :], dstate[:, :, 0, :],
                                        ALU.add).then_inc(s_mid, 1)
                nc.gpsimd.tensor_tensor(state[1 - p][:, :, 0, :], state[p][:, :, 0, :], dstate[:, :, 1, :],
                                        ALU.add).then_inc(s_next, 1)
                if mix:
                    mix_norms(c - 1)
                if not last:
                    norm_x(c + 1, 1 - p)
                if mix:
                    square_k(c - 1)
                if not last:
                    add_bo(c + 1, 1 - p)
                if mix:
                    finish(c - 1)

            def mix_only(m, p):
                mix_norms(m)
                square_k(m)
                finish(m)

            pool.wait_ge(weights_in, 16 * WEIGHT_DMAS)
            pool.wait_ge(x_loaded, 16)
            pool.wait_ge(dve_const, 1)
            norm_x(0, 0)
            add_bo(0, 0)
            steps(pool, attention_and_mix, mix_only)

        @block.tensor
        def _(pe):
            mm, tr = nc.tensor.matmul, nc.tensor.transpose
            pe.wait_ge(pool_const, 1)
            pe.wait_ge(weights_in, 16 * WEIGHT_DMAS)
            tr(ps_x[1][0:64, 0:64], wc_in[0:64, :], ident[0:64, 0:64])
            for i, w in enumerate((wk_in, wv_in)):
                for k in range(KD):
                    tr(ps_x[0][0:64, i * D + k * P:i * D + (k + 1) * P], w[:, k, :], ident[:])
            for i, b in enumerate((ps_w[0], ps_w[1], ps_y[0])):
                for k in range(KD):
                    for n in range(KD):
                        last = tr(b[:, (k * KD + n) * P:(k * KD + n + 1) * P], ffn_in[i][:, n, k * P:(k + 1) * P], ident[:])
            last.then_inc(prep_ps, 1)
            pe.wait_ge(prep_sb, 1)
            mm(ps_x[1][0:64, 128:128 + KV], wcT[0:64, :], we_in[0:64, :], start=True, stop=True).then_inc(prep_ps, 1)
            pe.wait_ge(prep_sb, 2)
            pe.wait_ge(bias_lhs, 1)
            for i in range(2):
                for k in range(KD):
                    mm(ps_y[1][:, (k * 2 + i) * KV:(k * 2 + i + 1) * KV], wkvT[0:64, i, k * P:(k + 1) * P],
                       cewe[0:64, :], start=True, stop=True)
            for i in range(2):
                last = mm(ps_y[1][:, 256 + i * KV:256 + (i + 1) * KV], bkv_lhs[0:64, i, :], cewe[0:64, :],
                          start=True, stop=True)
            last.then_inc(prep_ps, 1)
            pe.wait_ge(prep_sb, 3)

            def transpose_a(c, p):
                pe.wait_ge(s_a, 4 * c + 4)
                if not first(c):
                    pe.wait_ge(s_pr, 8 * c)
                for k in range(KD):
                    for b in range(NB):
                        last = tr(ps_z[k][:, b * P:(b + 1) * P], a_tok[p][:, b, k * P:(k + 1) * P], ident[:])
                    last.then_inc(s_aT_ps, 1)

            def project(c):
                pe.wait_ge(s_aT, 2 * c + 2)
                if not first(c):
                    pe.wait_ge(s_oT, 2 * c)
                for b in range(NB):
                    for k in range(KD):
                        last = mm(ps_z[0][:, b * P:(b + 1) * P], aT[:, k, b * P:(b + 1) * P], wkv_sb[:, k, :],
                                  start=(k == 0), stop=(k == KD - 1))
                last.then_inc(s_kv_ps, 1)
                for a in range(2):
                    for k in range(KD):
                        last = mm(ps_y[a][:, :], wq_sb[:, k, a, :], aT[:, k, :], start=(k == 0), stop=(k == KD - 1))
                    last.then_inc(s_q_ps, 1)

            def out_projection(m):
                pe.wait_ge(s_oT, 2 * m + 2)
                pe.wait_ge(s_gt, 2 * m + 1)
                for b in range(NB):
                    for a in range(2):
                        last = mm(ps_w[b // 2][:, (b % 2) * D:(b % 2 + 1) * D], oT[:, a, b, :, :], wo_sb[:, a, :],
                                  start=(a == 0), stop=(a == 1))
                    if b % 2:
                        last.then_inc(s_y_ps, 1)

            def keys(c):
                pe.wait_ge(s_kf, 2 * c + 2)
                for b in range(NB):
                    last = tr(ps_x[0][:, b * P:(b + 1) * P], kf[:, b * G:(b + 1) * G, :, :], ident[:])
                last.then_inc(s_kT_ps, 1)
                for b in range(NB):
                    last = mm(ps_x[1][:, b * P:(b + 1) * P], kf[:, b * G:(b + 1) * G, :, :], tri[:], start=True, stop=True)
                last.then_inc(s_ks_ps, 1)
                if not first(c):
                    pe.wait_ge(s_y, 2 * c)
                pe.wait_ge(s_kv, 5 * c + 5)
                for b in range(NB):
                    last = mm(ps_w[1][:, b * P:(b + 1) * P], kf[:, b * G:(b + 1) * G, :, :], v_half[:, b, :, :],
                              start=True, stop=True)
                last.then_inc(s_dS_ps, 1)

            def scores(c, p, b):
                if b == 0:
                    pe.wait_ge(s_kT, 2 * c + 2)
                    pe.wait_ge(s_qf, 2 * c + 2)
                else:
                    pe.wait_ge(s_pr, 8 * c + 2 * b)
                for pair in range(2):
                    if pair:
                        from_state(c, p, b, 0)
                        pe.wait_ge(s_sc, 16 * c + 4 * b + 2)
                    for g in (2 * pair, 2 * pair + 1):
                        for j in range(2):
                            for u in range(2):
                                rows, t0 = slice(32 * g, 32 * g + 32), b * P + HALF * u
                                col = (pair * 2 + j) * P
                                last = mm(ps_z[g % 2][HALF * u:HALF * u + HALF, col:col + P], kfT[rows, j, t0:t0 + HALF],
                                          qf[rows, :, t0:t0 + HALF], start=True, stop=True, skip_group_check=True)
                        last.then_inc(s_sc, 1)

            def from_state(c, p, b, u):
                if b == 0 and u == 0:
                    pe.wait_ge(s_mid, c + 1)
                t0 = b * P + HALF * u
                mm(ps_y[u][:, b * P:(b + 1) * P], state[p][:, b, u, :], qf[:, :, t0:t0 + HALF], start=(b == 0),
                   stop=False, skip_group_check=True)

            def outputs(c, p, b):
                pe.wait_ge(s_pr, 8 * c + 2 * b + 2)
                from_state(c, p, b, 1)
                cols = slice(b * P, (b + 1) * P)
                for j in range(2):
                    for u in range(2):
                        rows = slice(HALF * u, HALF * u + HALF)
                        for g in range(G):
                            col = (g // 2 * 2 + j) * P
                            last = mm(ps_y[u][32 * g:32 * g + 32, cols], v_pad[rows, j, b, g, :, :],
                                      probs[rows, b % 2, g % 2, col:col + P], start=False, stop=(j == 1),
                                      skip_group_check=True)
                last.then_inc(s_o, 1)

            def denominators(c):
                pe.wait_ge(s_prod, c + 1)
                for a in range(2):
                    last = mm(ps_x[0][32 * a:32 * a + 32, :], head_ones[:], prod[:, a, :], start=True, stop=True)
                last.then_inc(s_den_ps, 1)

            def denominators_by_token(c):
                pe.wait_ge(s_denT, c + 1)
                for b in range(NB):
                    last = tr(ps_x[1][:, b * P:(b + 1) * P], denT[:, b * P:(b + 1) * P], ident[:])
                last.then_inc(s_dtok_ps, 1)

            def reciprocals(c):
                pe.wait_ge(s_rden, c + 1)
                for b in range(NB):
                    last = tr(ps_x[0][0:16, b * P:(b + 1) * P], rden[:, b, :], ident[:])
                last.then_inc(s_rT_ps, 1)

            def spread_reciprocals(c):
                pe.wait_ge(s_rT, c + 1)
                for a in range(2):
                    mm(ps_x[a][:, :], spread[0:16, a, :], rdenT[0:16, :], start=True, stop=True).then_inc(s_rb_ps, 1)

            def transpose_z(m, c):
                pe.wait_ge(s_z, 4 * m + 4)
                if c is not None:
                    pe.wait_ge(s_dS, c + 1)
                for k in range(KD):
                    for b in range(NB):
                        last = tr(ps_w[k][:, b * P:(b + 1) * P], z_tok[:, b, k * P:(k + 1) * P], ident[:])
                    last.then_inc(s_zT_ps, 1)

            def mix_k(m):
                pe.wait_ge(s_xk, 2 * m + 2)
                for n in range(2):
                    for k in range(KD):
                        last = mm(ps_w[n][:, :], wkT[:, k, n * P:(n + 1) * P], xk[:, k, :, :], start=(k == 0),
                                  stop=(k == KD - 1))
                    last.then_inc(s_k_ps, 1)

            def mix_r(m, c):
                pe.wait_ge(s_xr, 2 * m + 2)
                if c is not None:
                    pe.wait_ge(s_rb, 2 * c + 2)
                elif not first(m):
                    pe.wait_ge(s_th, 2 * m)
                for b in range(NB):
                    for k in range(KD):
                        last = mm(ps_x[b // 2][:, (b % 2) * D:(b % 2 + 1) * D], xr[:, k, b, :], wrT[:, k, :],
                                  start=(k == 0), stop=(k == KD - 1))
                    if b % 2:
                        last.then_inc(s_r_ps, 1)

            def mix_v(m):
                pe.wait_ge(s_ka, 2 * m + 2)
                for b in range(NB):
                    for k in range(KD):
                        last = mm(ps_w[b // 2][:, (b % 2) * D:(b % 2 + 1) * D], k_act[:, k, b * P:(b + 1) * P],
                                  wvT[:, k, :], start=(k == 0), stop=(k == KD - 1))
                    if b % 2:
                        last.then_inc(s_v_ps, 1)

            def attention_and_mix(c, p, mix, last):
                project(c)
                if mix:
                    out_projection(c - 1)
                keys(c)
                scores(c, p, 0)
                denominators(c)
                scores(c, p, 1)
                outputs(c, p, 0)
                denominators_by_token(c)
                scores(c, p, 2)
                outputs(c, p, 1)
                reciprocals(c)
                scores(c, p, 3)
                outputs(c, p, 2)
                outputs(c, p, 3)
                spread_reciprocals(c)
                if mix:
                    transpose_z(c - 1, c)
                if not last:
                    transpose_a(c + 1, 1 - p)
                if mix:
                    mix_k(c - 1)
                    mix_r(c - 1, c)
                    mix_v(c - 1)

            def mix_only(m, p):
                out_projection(m)
                transpose_z(m, None)
                mix_k(m)
                mix_r(m, None)
                mix_v(m)

            transpose_a(0, 0)
            steps(pe, attention_and_mix, mix_only)

        @block.scalar
        def _(act):
            def copy(dst, src, **kw):
                return nc.scalar.activation(dst, src, ACT.Copy, **kw)

            act.wait_ge(prep_ps, 1)
            copy(wcT[0:64, :], ps_x[1][0:64, 0:64])
            copy(wkvT[0:64, :, :].rearrange("p i n -> p (i n)"), ps_x[0][0:64, :]).then_inc(prep_sb, 1)
            act.wait_ge(prep_ps, 2)
            copy(cewe[0:64, :], ps_x[1][0:64, 128:128 + KV]).then_inc(prep_sb, 1)
            copy(wrT[:].rearrange("p k n -> p (k n)"), ps_w[0][:, :])
            copy(wkT[:].rearrange("p k n -> p (k n)"), ps_w[1][:, :])
            copy(wvT[:].rearrange("p k n -> p (k n)"), ps_y[0][:, :], scale=0.5)
            act.wait_ge(prep_ps, 3)
            copy(wkv_sb[:].rearrange("p k n -> p (k n)"), ps_y[1][:, 0:256])
            copy(bkv_bc[:], ps_y[1][:, 256:384]).then_inc(prep_sb, 1)

            def a_out(c):
                for k in range(KD):
                    act.wait_ge(s_aT_ps, 2 * c + k + 1)
                    copy(aT[:, k, :], ps_z[k][:, :]).then_inc(s_aT, 1)

            def attention_and_mix(c, p, mix, last):
                act.wait_ge(s_kv, 5 * c + 1)
                nc.scalar.activation(ek[:], kb[:], ACT.Exp).then_inc(s_ek, 1)
                for a in range(2):
                    act.wait_ge(s_q_ps, 2 * c + a + 1)
                    nc.scalar.activation(eq[:, a, :], ps_y[a][:, :], ACT.Relu, bias=neg_bq[:, a:a + 1],
                                         scale=-1.0).then_inc(s_nq, 1)
                for a in range(2):
                    act.wait_ge(s_nq, 2 * c + a + 1)
                    nc.scalar.activation(eq[:, a, :], eq[:, a, :], ACT.Exp, scale=-1.0).then_inc(s_eq, 1)
                act.wait_ge(s_kT_ps, c + 1)
                for j in range(2):
                    copy(kfT[:, j, :], ps_x[0][:, :], scale=row_mask[:, j:j + 1]).then_inc(s_kT, 1)
                act.wait_ge(s_ks_ps, c + 1)
                if not first(c):
                    act.wait_ge(s_carry, c)
                for b in range(NB):
                    nc.scalar.activation(ksum[:, b * P:(b + 1) * P], ps_x[1][:, b * P:(b + 1) * P], ACT.Identity,
                                         bias=ksum_carry[:, b:b + 1]).then_inc(s_ks, 1)
                act.wait_ge(s_ks, 4 * c + 4)
                copy(ksum_carry[:], ksum[:].rearrange("p (b t) -> p b t", b=NB)[:, :, P - 1]).then_inc(s_carry, 1)
                act.wait_ge(s_den_ps, c + 1)
                copy(denT[0:64, :], ps_x[0][0:64, :]).then_inc(s_denT, 1)
                act.wait_ge(s_rT_ps, c + 1)
                copy(rdenT[0:16, :], ps_x[0][0:16, :]).then_inc(s_rT, 1)
                if mix:
                    normalise_z(c - 1)
                for a in range(2):
                    act.wait_ge(s_rb_ps, 2 * c + a + 1)
                    copy(rden_bc[:, a, :], ps_x[a][:, :]).then_inc(s_rb, 1)
                if mix:
                    shift_z(c - 1)
                if not last:
                    a_out(c + 1)
                if mix:
                    channel(c - 1)

            def normalise_z(m):
                act.wait_ge(s_rs2, 2 * m + 2)
                act.wait_ge(s_nb, m + 1)
                for b in range(NB):
                    nc.scalar.activation(z_tok[:, b, :], x2_tok[:, b, :], ACT.Identity, bias=nbias2[:, b:b + 1],
                                         scale=rstd2[:, b:b + 1]).then_inc(s_z, 1)

            def shift_z(m):
                copy(zT[:, :, :, 0], zT[:, :, :, P]).then_inc(s_zcar, 1)
                act.wait_ge(s_zcar, m + 1)
                for k in range(KD):
                    act.wait_ge(s_zT_ps, 2 * m + k + 1)
                    copy(zT[:, k, :, 1:P + 1], ps_w[k][:, :].rearrange("p (b t) -> p b t", b=NB)).then_inc(s_zT, 1)

            def channel(m):
                for n in range(2):
                    act.wait_ge(s_k_ps, 2 * m + n + 1)
                    nc.scalar.activation(relu_k[:, n, :], ps_w[n][:, :], ACT.Relu).then_inc(s_rl, 1)
                for i in range(2):
                    act.wait_ge(s_r_ps, 2 * m + i + 1)
                    nc.scalar.activation(tanh_r[:, i, :], ps_x[i][:, :], ACT.Tanh, scale=0.5).then_inc(s_th, 1)

            def mix_only(m, p):
                normalise_z(m)
                shift_z(m)
                channel(m)

            act.wait_ge(dve_const, 1)
            a_out(0)
            steps(act, attention_and_mix, mix_only)

        @block.vector
        def _(dve):
            V = nc.vector
            for t in (v_pad, v_half, zT, ksum_carry, state[0], denT):
                V.memset(t[:], 0.0)
            V.memset(ones64[:], 1.0).then_inc(s_gt, 1)
            dve.wait_ge(pool_const, 1)
            dve.wait_ge(weights_in, 16 * WEIGHT_DMAS)
            for j in range(2):
                V.tensor_reduce(row_mask[:, j:j + 1], head_ones[:, j:8:2], AX_X, ALU.add)
            V.tensor_scalar(neg_bq[:], bq_col[:], -1.0, None, ALU.mult)
            V.tensor_scalar(bq_1[:], bq_col[:], 1.0, None, ALU.add).then_inc(dve_const, 1)
            dve.wait_ge(dve_const, 1)
            for i in range(2):
                last = V.tensor_scalar(bkv_lhs[0:64, i, :], ones64[0:64, :], bkv_col[0:64, i:i + 1], None, ALU.mult)
            last.then_inc(bias_lhs, 1)

            def row_stats(src, stats, mv, done, c):
                for b in range(NB):
                    V.bn_stats(stats[:, b, :], src[:, b, :]).then_inc(done, 1)
                dve.wait_ge(done, 8 * c + NB)
                V.memset(wait_carrier[:], 0.0)
                for b in range(NB):
                    V.bn_aggr(mv[:, b, :], stats[:, b, :]).then_inc(done, 1)

            def norm_x(c, p):
                dve.wait_ge(x_loaded, 16 * c + 16)
                row_stats(x_in, stats0, mv0, s_st0, c)

            def norm_x_scale(c, p):
                dve.wait_ge(s_st0, 8 * c + 8)
                dve.wait_ge(s_rs0, 2 * c + 2)
                for b in range(NB):
                    V.tensor_scalar(a_tok[p][:, b, :], x_in[:, b, :], mv0[:, b, 0:1], rstd0[:, b:b + 1], ALU.subtract,
                                    ALU.mult).then_inc(s_a, 1)

            def keys_values(c):
                dve.wait_ge(s_kv_ps, c + 1)
                kv = ps_z[0][:, :].rearrange("p (b n) -> p b n", b=NB)
                bias = bkv_bc[:].unsqueeze(1).to_broadcast([P, NB, 2 * KV])
                V.tensor_tensor(kb[:], kv[:, :, 0:KV], bias[:, :, 0:KV], ALU.add).then_inc(s_kv, 1)
                V.tensor_tensor(v_tok[:], kv[:, :, KV:2 * KV], bias[:, :, KV:2 * KV], ALU.add).then_inc(s_kv, 1)
                dve.wait_ge(s_kv, 5 * c + 2)
                V.tensor_copy(v_half[:, :, 1, :], v_tok[:])
                V.tensor_copy(v_half[0:HALF, :, 0, :], v_tok[0:HALF]).then_inc(s_kv, 1)
                for j in range(2):
                    V.tensor_copy(v_pad[:, j, :, :, j, :].rearrange("p b g d -> p (b g) d"),
                                  v_tok[:].rearrange("p b (g d) -> p (b g) d", d=HD)).then_inc(s_kv, 1)

            def features(c):
                dve.wait_ge(s_ek, c + 1)
                V.tensor_scalar(ek[:], ek[:], 1.0, None, ALU.min).then_inc(s_ekm, 1)
                dve.wait_ge(s_ekm, c + 1)
                for j in range(2):
                    V.scalar_tensor_tensor(out=kf[:, :, j, :], in0=kb[:].rearrange("p b (g d) -> p (b g) d", d=HD),
                                           scalar=1.0, in1=ek[:].rearrange("p b (g d) -> p (b g) d", d=HD),
                                           op0=ALU.add, op1=ALU.max).then_inc(s_kf, 1)
                for a in range(2):
                    dve.wait_ge(s_eq, 2 * c + a + 1)
                    V.scalar_tensor_tensor(out=qf[:, a, :], in0=ps_y[a][:, :], scalar=bq_1[:, a:a + 1], in1=eq[:, a, :],
                                           op0=ALU.add, op1=ALU.max).then_inc(s_qf, 1)

            def add_residual(m, p):
                dve.wait_ge(s_ab, m + 1)
                for i in range(2):
                    dve.wait_ge(s_y_ps, 2 * m + i + 1)
                    V.tensor_tensor(y_tok[:, 2 * i:2 * i + 2, :], ps_w[i][:, :].rearrange("p (b d) -> p b d", b=2),
                                    a_tok[p][:, 2 * i:2 * i + 2, :], ALU.add).then_inc(s_y, 1)
                dve.wait_ge(s_y, 2 * m + 2)
                row_stats(y_tok, stats1, mv1, s_st1, m)

            def state_increment(c):
                dve.wait_ge(s_dS_ps, c + 1)
                if not first(c):
                    dve.wait_ge(s_next, c)
                V.tensor_tensor(dstate[:].rearrange("p b u (g j d) -> p (b u g) j d", g=G, j=2),
                                ps_w[1][:, :].rearrange("p (r d) -> p r d", d=HD).unsqueeze(2).to_broadcast([P, 32, 2, HD]),
                                head_rep[:].rearrange("p r (g j d) -> p (r g) j d", g=G, j=2),
                                ALU.mult).then_inc(s_dS, 1)

            def denominator_terms(c):
                dve.wait_ge(s_ks, 4 * c + 4)
                dve.wait_ge(s_qf, 2 * c + 2)
                V.tensor_tensor(prod[:], qf[:], ksum[:].unsqueeze(1).to_broadcast([P, 2, T]), ALU.mult).then_inc(s_prod, 1)

            def mask(c, b):
                if not (first(c) and b < 2):
                    dve.wait_ge(s_o, 4 * c + b - 1)
                for z in range(2):
                    dve.wait_ge(s_sc, 16 * c + 4 * b + z + 3)
                    V.tensor_tensor(probs[:, b % 2, z, :].rearrange("p (r s) -> p r s", s=HALF),
                                    ps_z[z][:, :].rearrange("p (r s) -> p r s", s=HALF),
                                    causal[:].unsqueeze(1).to_broadcast([P, 8, HALF]), ALU.mult).then_inc(s_pr, 1)

            def second_residual(m, p):
                dve.wait_ge(s_st1, 8 * m + 8)
                for b in range(NB):
                    V.scalar_tensor_tensor(out=t_tok[:, b, :], in0=y_tok[:, b, :], scalar=mv1[:, b, 0:1], in1=gamma_bc[:],
                                           op0=ALU.subtract, op1=ALU.mult).then_inc(s_t, 1)
                dve.wait_ge(s_rs1, 2 * m + 2)
                dve.wait_ge(s_xb, m + 1)
                dve.wait_ge(s_out, 2 * m + 1)
                for b in range(NB):
                    dve.wait_ge(s_t, 4 * m + b + 1)
                    V.scalar_tensor_tensor(out=x2_tok[:, b, :], in0=t_tok[:, b, :], scalar=rstd1[:, b:b + 1],
                                           in1=xb_tok[p][:, b, :], op0=ALU.mult, op1=ALU.add).then_inc(s_x2, 1)

            def second_stats(m):
                dve.wait_ge(s_x2, 4 * m + 4)
                row_stats(x2_tok, stats2, mv2, s_st2, m)

            def second_bias(m):
                dve.wait_ge(s_st2, 8 * m + 8)
                dve.wait_ge(s_rs2, 2 * m + 2)
                V.scalar_tensor_tensor(out=nbias2[:], in0=mv2[:, :, 0], scalar=-1.0, in1=rstd2[:], op0=ALU.mult,
                                       op1=ALU.mult).then_inc(s_nb, 1)

            def reciprocal(c):
                dve.wait_ge(s_dtok_ps, c + 1)
                V.tensor_scalar(den[:].rearrange("p b (a n) -> p b a n", a=2),
                                ps_x[1][:, :].rearrange("p (b a n) -> p b a n", b=NB, a=4)[:, :, 0:2, 0:8],
                                DEN_EPS, None, ALU.add).then_inc(s_den, 1)
                dve.wait_ge(s_den, c + 1)
                V.reciprocal(rden[:], den[:]).then_inc(s_rden, 1)

            def divide(c):
                dve.wait_ge(s_o, 4 * c + 4)
                dve.wait_ge(s_rb, 2 * c + 2)
                for u in range(2):
                    V.tensor_tensor(oT[:, :, :, u, :], ps_y[u][:, :].rearrange("p (b a s) -> p a b s", b=NB, a=2),
                                    rden_bc[:].rearrange("p a (b u s) -> p a b u s", b=NB, u=2)[:, :, :, u, :],
                                    ALU.mult).then_inc(s_oT, 1)

            def token_shift(m):
                dve.wait_ge(s_zT, 2 * m + 2)
                now, before = zT[:, :, :, 1:P + 1], zT[:, :, :, 0:P]
                V.tensor_tensor(dz[:], now.rearrange("p k b t -> p (k b) t"), before.rearrange("p k b t -> p (k b) t"),
                                ALU.subtract).then_inc(s_dz, 1)
                dve.wait_ge(s_dz, m + 1)
                for dst, mu, done in ((xk, mu_k_col, s_xk), (xr, mu_r_col, s_xr)):
                    for k in range(KD):
                        V.scalar_tensor_tensor(out=dst[:, k], in0=dz[:, k * NB:(k + 1) * NB, :], scalar=mu[:, k:k + 1],
                                               in1=zT[:, k, :, 0:P], op0=ALU.mult, op1=ALU.add).then_inc(done, 1)

            def gate(m):
                for i in range(2):
                    dve.wait_ge(s_th, 2 * m + i + 1)
                    dve.wait_ge(s_v_ps, 2 * m + i + 1)
                    V.scalar_tensor_tensor(out=gated[:, i, :], in0=tanh_r[:, i, :], scalar=1.0, in1=ps_w[i][:, :],
                                           op0=ALU.add, op1=ALU.mult).then_inc(s_gt, 1)

            def attention_and_mix(c, p, mix, last):
                keys_values(c)
                features(c)
                if mix:
                    add_residual(c - 1, 1 - p)
                state_increment(c)
                denominator_terms(c)
                mask(c, 0)
                if mix:
                    second_residual(c - 1, 1 - p)
                    second_stats(c - 1)
                mask(c, 1)
                if not last:
                    norm_x(c + 1, 1 - p)
                if mix:
                    second_bias(c - 1)
                mask(c, 2)
                reciprocal(c)
                if not last:
                    norm_x_scale(c + 1, 1 - p)
                mask(c, 3)
                divide(c)
                if mix:
                    token_shift(c - 1)
                    gate(c - 1)

            def mix_only(m, p):
                add_residual(m, p)
                second_residual(m, p)
                second_stats(m)
                second_bias(m)
                token_shift(m)
                gate(m)

            norm_x(0, 0)
            norm_x_scale(0, 0)
            dve.wait_ge(prep_sb, 3)
            steps(dve, attention_and_mix, mix_only)


_INS = ['L0_attn_x', 'L0_attn_Wq', 'L0_attn_bq', 'L0_attn_Wk', 'L0_attn_bk', 'L0_attn_Wv', 'L0_attn_bv', 'L0_attn_Wc',
        'L0_attn_We', 'L0_attn_Wo', 'L0_attn_bo', 'L0_attn_gamma', 'L0_attn_beta', 'L0_ffn_W_r', 'L0_ffn_W_k',
        'L0_ffn_W_v', 'L0_ffn_mu_r', 'L0_ffn_mu_k']


def kernel(**inputs):
    import numpy as _np
    import concourse.bacc as _bacc
    from concourse import mybir as _mybir
    from concourse.bass_utils import run_bass_kernel_spmd as _run

    nc = _bacc.Bacc("TRN2", target_bir_lowering=False, num_devices=1)
    arrays, args = {}, []
    for name in _INS:
        a = _np.ascontiguousarray(inputs[name])
        arrays[f"in_{name}_dram"] = a
        args.append(nc.dram_tensor(f"in_{name}_dram", a.shape, _mybir.dt.from_np(a.dtype), kind="ExternalInput").ap())
    args.append(nc.dram_tensor("out_dram", inputs['L0_attn_x'].shape, _mybir.dt.float32, kind="ExternalOutput").ap())
    build(nc, *args)
    r = _run(nc, [arrays], core_ids=[0])
    return r.results[0]["out_dram"]
```

```python
from contextlib import ExitStack

import concourse.bass as bass
from concourse import mybir

P = 128
ALU = mybir.AluOpType
ACT = mybir.ActivationFunctionType
F32 = mybir.dt.float32
F32R = mybir.dt.float32r
AX_X = mybir.AxisListType.X

LN_EPS = 1e-5
DEN_EPS = 1e-6


def build(nc, x, wq, bq, wk, bk, wv, bv, wc, we, wo, bo, gamma, beta, w_r, w_k, w_v, mu_r, mu_k, out):
    NB, S, D = x.shape
    NC = S // P
    KD = D // P
    G, HD = 4, 16
    KV = G * HD
    HALF = P // 2
    T = NB * P
    assert D == 256 and NB == 4 and KV == wk.shape[1] and NC % 2 == 0

    def chunk_at(dram, start):
        return dram.rearrange("b t d -> b (t d)")[:, bass.ds(start, P * D)].rearrange("b (t d) -> t b d", d=D)

    with ExitStack() as ctx:
        def sb(name, *shape):
            return ctx.enter_context(nc.sbuf_tensor(name, [P, *shape], F32))

        def sem(name):
            return ctx.enter_context(nc.semaphore(name))

        def bank(name):
            return ctx.enter_context(nc.psum_tensor(name, [P, 512], F32))

        ps_x = [bank("ps_x0"), bank("ps_x1")]
        ps_y = [bank("ps_y0"), bank("ps_y1")]
        ps_z = [bank("ps_z0"), bank("ps_z1")]
        ps_w = [bank("ps_w0"), bank("ps_w1")]

        ident = sb("ident", P)
        tri = sb("tri", P)
        causal = sb("causal", HALF)
        head_ones = sb("head_ones", 32)
        head_rep = sb("head_rep", 2 * NB, P)
        spread = sb("spread", 2, P)
        spread_r = ctx.enter_context(nc.sbuf_tensor("spread_r", [P, 2, P], F32R))
        row_mask = sb("row_mask", 2)
        neg_half, ln_eps = sb("neg_half", NB), sb("ln_eps", NB)
        ones64, wait_carrier = sb("ones64", P), sb("wait_carrier", 1)

        wc_in, we_in, wk_in, wv_in = sb("wc_in", 64), sb("we_in", 64), sb("wk_in", KD, KV), sb("wv_in", KD, KV)
        bkv_col = sb("bkv_col", 2)
        ffn_in = [sb(f"ffn_in{i}", KD, D) for i in range(3)]
        wq_sb = sb("wq_sb", KD, 2, P)
        wo_sb = sb("wo_sb", 2, D)
        bq_col, neg_bq, bq_1 = sb("bq_col", 2), sb("neg_bq", 2), sb("bq_1", 2)
        gamma_bc, beta_bc, bo_bc = sb("gamma_bc", D), sb("beta_bc", D), sb("bo_bc", D)
        mu_r_col, mu_k_col = sb("mu_r_col", KD), sb("mu_k_col", KD)
        wcT, wkvT, cewe, bkv_lhs = sb("wcT", 64), sb("wkvT", 2, D), sb("cewe", KV), sb("bkv_lhs", 2, P)
        wkv_sb, bkv_bc = sb("wkv_sb", KD, 2 * KV), sb("bkv_bc", 2 * KV)
        wrT, wkT, wvT = sb("wrT", KD, D), sb("wkT", KD, D), sb("wvT", KD, D)

        x_in = [sb(f"x_in{i}", NB, D) for i in range(2)]
        a_tok = sb("a_tok", NB, D)
        abo_tok = [sb(f"abo_tok{i}", NB, D) for i in range(2)]
        xb_tok = [sb(f"xb_tok{i}", NB, D) for i in range(2)]
        stats0, mv0, rstd0 = sb("stats0", NB, 6), sb("mv0", NB, 2), sb("rstd0", NB)
        aT = sb("aT", KD, T)
        eq, qf = sb("eq", 2, T), [sb(f"qf{i}", 2, T) for i in range(2)]
        kb, ek = sb("kb", NB, KV), sb("ek", NB, KV)
        v_tok = sb("v_tok", NB, KV)
        v_pad = [sb(f"v_pad{i}", 2, NB, G, 2, HD) for i in range(2)]
        v_half = sb("v_half", NB, 2, KV)
        kf = sb("kf", NB * G, 2, HD)
        kfT = sb("kfT", 2, T)
        ksum, ksum_carry = sb("ksum", T), sb("ksum_carry", NB)
        prod = sb("prod", 2, T)
        denT, den, rden, rdenT, rden_bc = sb("denT", T), sb("den", NB, 16), sb("rden", NB, 16), ctx.enter_context(nc.sbuf_tensor("rdenT", [P, T], F32R)), sb("rden_bc", 2, T)
        rden_parts = sb("rden_parts", NB, 2, 16)
        dstate = sb("dstate", NB, 2, P)
        state = [sb(f"state{i}", NB, 2, P) for i in range(2)]
        probs = sb("probs", 2, 2, 512)
        oT = sb("oT", 2, NB, 2, HALF)
        y_tok, t_tok, x2_tok, z_tok = sb("y_tok", NB, D), sb("t_tok", NB, D), sb("x2_tok", NB, D), sb("z_tok", NB, D)
        stats1, mv1, rstd1 = sb("stats1", NB, 6), sb("mv1", NB, 2), sb("rstd1", NB)
        stats2, mv2, rstd2, nbias2 = sb("stats2", NB, 6), sb("mv2", NB, 2), sb("rstd2", NB), sb("nbias2", NB)
        zT = sb("zT", KD, NB, P + 1)
        dz, xr, xk = sb("dz", KD * NB, P), sb("xr", KD, NB, P), sb("xk", KD, NB, P)
        relu_k, k_act = sb("relu_k", 2, T), sb("k_act", 2, T)
        tanh_r, gated, out_tok = sb("tanh_r", 2, 512), sb("gated", 2, 512), sb("out_tok", NB, D)

        weights_in, out_stored = sem("weights_in"), sem("out_stored")
        x_loaded = [sem("x_loaded0"), sem("x_loaded1")]
        pool_const, dve_const, prep_ps, prep_sb = sem("pool_const"), sem("dve_const"), sem("prep_ps"), sem("prep_sb")
        pool_link, bias_lhs = sem("pool_link"), sem("bias_lhs")
        s_st0, s_rs0, s_a, s_xb, s_ab = sem("stats0_done"), sem("rstd0_done"), sem("a_ready"), sem("xbeta_ready"), sem("abo_ready")
        s_aT_ps, s_aT = sem("aT_ps"), sem("aT_ready")
        s_q_ps, s_nq, s_eq, s_qf = sem("q_ps"), sem("negq"), sem("expq"), sem("qf_ready")
        s_kv_ps, s_kv, s_ek, s_ekm, s_kf = sem("kv_ps"), sem("kv_ready"), sem("expk"), sem("expk_min"), sem("kf_ready")
        s_kT_ps, s_kT, s_ks_ps, s_ks, s_carry = sem("kT_ps"), sem("kT_ready"), sem("ksum_ps"), sem("ksum_ready"), sem("carry_ready")
        s_dS_ps, s_dS, s_mid, s_next = sem("dstate_ps"), sem("dstate_ready"), sem("state_mid"), sem("state_next")
        s_prod, s_den_ps, s_denT, s_dtok_ps, s_den, s_rden = (
            sem("prod_ready"), sem("den_ps"), sem("denT_ready"), sem("dtok_ps"), sem("den_ready"), sem("rden_ready"))
        s_rparts = sem("rden_high_ready")
        s_rT_ps, s_rT, s_rb_ps, s_rb = sem("rdenT_ps"), sem("rdenT_ready"), sem("rdenbc_ps"), sem("rdenbc_ready")
        s_sc, s_pr, s_o, s_oT = sem("scores_ps"), sem("probs_ready"), sem("o_ps"), sem("oT_ready")
        s_y_ps, s_y, s_st1, s_rs1, s_t, s_x2 = (
            sem("y_ps"), sem("y_ready"), sem("stats1_done"), sem("rstd1_done"), sem("t_ready"), sem("x2_ready"))
        s_st2, s_rs2, s_nb, s_z = sem("stats2_done"), sem("rstd2_done"), sem("nbias2_ready"), sem("z_ready")
        s_zT_ps, s_zcar, s_zT, s_dz, s_xk, s_xr = (
            sem("zT_ps"), sem("zshift_ready"), sem("zT_ready"), sem("dz_ready"), sem("xk_ready"), sem("xr_ready"))
        s_k_ps, s_rl, s_ka, s_r_ps, s_th, s_v_ps, s_gt, s_out = (
            sem("k_ps"), sem("relu_ready"), sem("kact_ready"), sem("r_ps"), sem("tanh_ready"), sem("v_ps"),
            sem("gated_ready"), sem("out_ready"))

        first = lambda c: isinstance(c, int) and c == 0
        within = lambda c: not isinstance(c, int) or c < NC

        def steps(eng, step, mix_only):
            step(0, 0, False, False)
            step(1, 1, True, False)
            with eng.Fori(0, NC // 2 - 2) as pair:
                step(2 * pair + 2, 0, True, False)
                step(2 * pair + 3, 1, True, False)
            step(NC - 2, 0, True, False)
            step(NC - 1, 1, True, True)
            mix_only(NC - 1, 1)

        block = ctx.enter_context(nc.Block())

        WEIGHT_DMAS = 0
        loads = [(wc_in[0:64, :], wc), (we_in[0:64, :], we),
                 (wk_in[:], wk.rearrange("(k p) n -> p k n", p=P)), (wv_in[:], wv.rearrange("(k p) n -> p k n", p=P)),
                 (bkv_col[0:64, 0:1], bk.rearrange("(n o) -> n o", o=1)),
                 (bkv_col[0:64, 1:2], bv.rearrange("(n o) -> n o", o=1))]
        for k in range(KD):
            for g in range(G):
                loads.append((wq_sb[:, k, :, 32 * g:32 * g + 32],
                              wq[k * P:(k + 1) * P, 64 * g:64 * g + 64].rearrange("p (a m) -> p a m", a=2)))
        for g in range(G):
            loads.append((bq_col[32 * g:32 * g + 32, :], bq[64 * g:64 * g + 64].rearrange("(a m) -> m a", a=2)))
        for w, dst in ((w_k, ffn_in[1]), (w_r, ffn_in[0]), (w_v, ffn_in[2])):
            loads.append((dst[:], w.rearrange("(k p) n -> p k n", p=P)))
        for g in range(G):
            loads.append((wo_sb[32 * g:32 * g + 32, :, :], wo[64 * g:64 * g + 64, :].rearrange("(a m) n -> m a n", a=2)))
        for v, dst in ((gamma, gamma_bc), (beta, beta_bc), (bo, bo_bc)):
            loads.append((dst[:], v.partition_broadcast(P)))
        for v, dst in ((mu_r, mu_r_col), (mu_k, mu_k_col)):
            loads.append((dst[:], v.rearrange("(k p) -> p k", p=P)))
        WEIGHT_DMAS = len(loads)

        @block.sync
        def _(sp):
            sp.sem_inc(out_stored, 16)
            def load(n, p):
                sp.dma_start(x_in[p][:], chunk_at(x, n * P * D)).then_inc(x_loaded[p], 16)

            def load_ahead(c, p):
                sp.wait_ge(s_xb, c + 1)
                sp.wait_ge(s_a, 4 * c + 4)
                load(c + 2, p)

            def store(m):
                sp.wait_ge(s_out, 2 * m + 3)
                sp.dma_start(chunk_at(out, m * P * D), out_tok[:]).then_inc(out_stored, 16)

            load(0, 0)
            with nc.allow_non_contiguous_dma(reason="bias and mixing vectors, one element a partition"):
                for dst, src in loads:
                    sp.dma_start(dst, src).then_inc(weights_in, 16)
            load(1, 1)
            load_ahead(0, 0)
            with sp.Fori(0, NC // 2 - 2) as pair:
                for i, p in ((1, 1), (2, 0)):
                    load_ahead(2 * pair + i, p)
                    store(2 * pair + i - 1)
            load_ahead(NC - 3, 1)
            for m in range(NC - 4, NC):
                store(m)
            sp.wait_ge(out_stored, 16 * NC + 16)

        @block.gpsimd
        def _(pool):
            links = [0]

            def link(ins):
                links[0] += 1
                ins.then_inc(pool_link, 1)
                pool.wait_ge(pool_link, links[0])

            link(nc.gpsimd.memset(ident[:], 0.0))
            link(nc.gpsimd.affine_select(out=ident[:], in_=ident[:], compare_op=ALU.not_equal, fill=1.0, base=0,
                                         pattern=[[-1, P]], channel_multiplier=1))
            link(nc.gpsimd.memset(tri[:], 1.0))
            link(nc.gpsimd.affine_select(out=tri[:], in_=tri[:], compare_op=ALU.is_ge, fill=0.0, base=0,
                                         pattern=[[1, P]], channel_multiplier=-1))
            link(nc.gpsimd.memset(causal[:], 1.0))
            for u in range(2):
                half = causal[HALF * u:HALF * u + HALF, :]
                link(nc.gpsimd.affine_select(out=half, in_=half, compare_op=ALU.is_ge, fill=0.0, base=0,
                                             pattern=[[1, HALF]], channel_multiplier=-1))
            link(nc.gpsimd.memset(head_ones[:], 1.0))
            link(nc.gpsimd.affine_select(out=head_ones[:], in_=head_ones[:], compare_op=ALU.is_ge, fill=0.0, base=0,
                                         pattern=[[-16, 32]], channel_multiplier=1))
            link(nc.gpsimd.affine_select(out=head_ones[:], in_=head_ones[:], compare_op=ALU.is_ge, fill=0.0, base=15,
                                         pattern=[[16, 32]], channel_multiplier=-1))
            link(nc.gpsimd.memset(head_rep[:], 1.0))
            rep = head_rep[:].rearrange("p r (n d) -> p r n d", d=HD)
            link(nc.gpsimd.affine_select(out=rep, in_=rep, compare_op=ALU.is_ge, fill=0.0, base=0,
                                         pattern=[[0, 2 * NB], [-16, 8], [0, HD]], channel_multiplier=1))
            link(nc.gpsimd.affine_select(out=rep, in_=rep, compare_op=ALU.is_ge, fill=0.0, base=15,
                                         pattern=[[0, 2 * NB], [16, 8], [0, HD]], channel_multiplier=-1))
            link(nc.gpsimd.memset(spread[:], 0.0))
            spr = spread[0:32, :, :].rearrange("p a (n d) -> p a n d", d=HD)
            for part in range(2):
                link(nc.gpsimd.affine_select(out=spr, in_=spr, compare_op=ALU.not_equal, fill=1.0, base=-16 * part,
                                             pattern=[[-8, 2], [-1, 8], [0, HD]], channel_multiplier=1))
            link(nc.gpsimd.memset(ln_eps[:], LN_EPS))
            nc.gpsimd.memset(out_tok[:, 0, 0:1], 0.0).then_inc(s_out, 1)
            nc.gpsimd.memset(neg_half[:], -0.5).then_inc(pool_const, 1)
            pool.wait_ge(pool_const, 1)

            def rstd(dst, mv, eps, stats_done, stats_value, done, value):
                pool.wait_ge(stats_done, stats_value)
                nc.gpsimd.tensor_tensor(dst[:], mv[:, :, 1], eps[:], ALU.add).then_inc(done, 1)
                pool.wait_ge(done, value)
                nc.gpsimd.tensor_tensor(dst[:], dst[:], neg_half[:], ALU.pow).then_inc(done, 1)

            def norm_x(n):
                rstd(rstd0, mv0, ln_eps, s_st0, 8 * n + 8, s_rs0, 2 * n + 1)

            def add_beta(n, p):
                if not isinstance(n, int) or n >= 2:
                    pool.wait_ge(s_x2, 4 * n - 4)
                nc.gpsimd.tensor_tensor(xb_tok[p][:], x_in[p][:], beta_bc[:].unsqueeze(1).to_broadcast([P, NB, D]),
                                        ALU.add).then_inc(s_xb, 1)

            def add_bo(c, p):
                pool.wait_ge(s_a, 4 * c + 4)
                if not isinstance(c, int) or c >= 2:
                    pool.wait_ge(s_y, 2 * c - 2)
                nc.gpsimd.tensor_tensor(abo_tok[p][:], a_tok[:], bo_bc[:].unsqueeze(1).to_broadcast([P, NB, D]),
                                        ALU.add).then_inc(s_ab, 1)

            def mix_norms(m):
                rstd(rstd1, mv1, ln_eps, s_st1, 8 * m + 8, s_rs1, 2 * m + 1)
                rstd(rstd2, mv2, ln_eps, s_st2, 8 * m + 8, s_rs2, 2 * m + 1)

            def finish(m):
                pool.wait_ge(out_stored, 16 * m + 16)
                for i in range(2):
                    pool.wait_ge(s_gt, 2 * m + i + 2)
                    nc.gpsimd.tensor_tensor(out_tok[:, 2 * i:2 * i + 2, :],
                                            gated[:, i].rearrange("p (b d) -> p b d", b=2),
                                            x2_tok[:, 2 * i:2 * i + 2, :], ALU.add).then_inc(s_out, 1)

            def states(n, p):
                pool.wait_ge(s_dS, n + 1)
                if not first(n):
                    pool.wait_ge(s_next, n)
                nc.gpsimd.tensor_tensor(state[p][:, :, 1, :], state[p][:, :, 0, :], dstate[:, :, 0, :],
                                        ALU.add).then_inc(s_mid, 1)
                nc.gpsimd.tensor_tensor(state[1 - p][:, :, 0, :], state[p][:, :, 0, :], dstate[:, :, 1, :],
                                        ALU.add).then_inc(s_next, 1)

            def step(c, p, mix, last):
                if mix:
                    mix_norms(c - 1)
                if not last:
                    add_bo(c + 1, 1 - p)
                    add_beta(c + 1, 1 - p)
                    states(c + 1, 1 - p)
                if within(c + 2):
                    norm_x(c + 2)
                if mix:
                    finish(c - 1)

            def mix_only(m, p):
                mix_norms(m)
                finish(m)

            pool.wait_ge(weights_in, 16 * WEIGHT_DMAS)
            pool.wait_ge(dve_const, 1)
            norm_x(0)
            norm_x(1)
            add_bo(0, 0)
            add_beta(0, 0)
            states(0, 0)
            steps(pool, step, mix_only)

        @block.tensor
        def _(pe):
            mm, tr = nc.tensor.matmul, nc.tensor.transpose
            pe.wait_ge(pool_const, 1)
            pe.wait_ge(weights_in, 16 * WEIGHT_DMAS)
            tr(ps_x[1][0:64, 0:64], wc_in[0:64, :], ident[0:64, 0:64])
            for i, w in enumerate((wk_in, wv_in)):
                for k in range(KD):
                    tr(ps_x[0][0:64, i * D + k * P:i * D + (k + 1) * P], w[:, k, :], ident[:])
            for i, b in enumerate((ps_w[0], ps_w[1], ps_y[0])):
                for k in range(KD):
                    for n in range(KD):
                        last = tr(b[:, (k * KD + n) * P:(k * KD + n + 1) * P], ffn_in[i][:, n, k * P:(k + 1) * P], ident[:])
            last.then_inc(prep_ps, 1)
            pe.wait_ge(prep_sb, 1)
            mm(ps_x[1][0:64, 128:128 + KV], wcT[0:64, :], we_in[0:64, :], start=True, stop=True).then_inc(prep_ps, 1)
            pe.wait_ge(prep_sb, 2)
            pe.wait_ge(bias_lhs, 1)
            for i in range(2):
                for k in range(KD):
                    mm(ps_y[1][:, (k * 2 + i) * KV:(k * 2 + i + 1) * KV], wkvT[0:64, i, k * P:(k + 1) * P],
                       cewe[0:64, :], start=True, stop=True)
            for i in range(2):
                last = mm(ps_y[1][:, 256 + i * KV:256 + (i + 1) * KV], bkv_lhs[0:64, i, :], cewe[0:64, :],
                          start=True, stop=True)
            last.then_inc(prep_ps, 1)
            pe.wait_ge(prep_sb, 3)

            def transpose_a(n):
                pe.wait_ge(s_a, 4 * n + 4)
                if not first(n):
                    pe.wait_ge(s_ks, 4 * n)
                for k in range(KD):
                    for b in range(NB):
                        last = tr(ps_x[k][:, b * P:(b + 1) * P], a_tok[:, b, k * P:(k + 1) * P], ident[:])
                    last.then_inc(s_aT_ps, 1)

            def queries(n, a):
                if a == 0:
                    pe.wait_ge(s_aT, 2 * n + 2)
                for k in range(KD):
                    last = mm(ps_x[a][:, :], wq_sb[:, k, a, :], aT[:, k, :], start=(k == 0), stop=(k == KD - 1))
                last.then_inc(s_q_ps, 1)

            def keys_values(n):
                pe.wait_ge(s_qf, 2 * n + 2)
                for b in range(NB):
                    for k in range(KD):
                        last = mm(ps_x[0][:, b * P:(b + 1) * P], aT[:, k, b * P:(b + 1) * P], wkv_sb[:, k, :],
                                  start=(k == 0), stop=(k == KD - 1))
                last.then_inc(s_kv_ps, 1)

            def out_projection(m, i):
                if i == 0:
                    pe.wait_ge(s_oT, 2 * m + 2)
                pe.wait_ge(s_gt, 2 * m + 1)
                for b in (2 * i, 2 * i + 1):
                    for a in range(2):
                        last = mm(ps_w[i][:, (b % 2) * D:(b % 2 + 1) * D], oT[:, a, b, :, :], wo_sb[:, a, :],
                                  start=(a == 0), stop=(a == 1))
                last.then_inc(s_y_ps, 1)

            def key_sums(n):
                pe.wait_ge(s_kf, 2 * n + 2)
                if not first(n):
                    pe.wait_ge(s_rb, 2 * n)
                for b in range(NB):
                    last = tr(ps_x[0][:, b * P:(b + 1) * P], kf[:, b * G:(b + 1) * G, :, :], ident[:])
                last.then_inc(s_kT_ps, 1)
                for b in range(NB):
                    last = mm(ps_x[1][:, b * P:(b + 1) * P], kf[:, b * G:(b + 1) * G, :, :], tri[:], start=True, stop=True)
                last.then_inc(s_ks_ps, 1)

            def state_increments(n):
                pe.wait_ge(s_kf, 2 * n + 2)
                pe.wait_ge(s_kv, 5 * n + 5)
                if not first(n):
                    pe.wait_ge(s_pr, 8 * n)
                for b in range(NB):
                    last = mm(ps_z[1][:, b * P:(b + 1) * P], kf[:, b * G:(b + 1) * G, :, :], v_half[:, b, :, :],
                              start=True, stop=True)
                last.then_inc(s_dS_ps, 1)

            def scores(c, p, b):
                if b == 0:
                    pe.wait_ge(s_kT, 2 * c + 2)
                    pe.wait_ge(s_mid, c + 1)
                    if not first(c):
                        pe.wait_ge(s_oT, 2 * c)
                else:
                    pe.wait_ge(s_pr, 8 * c + 2 * b)
                for pair in range(2):
                    if pair:
                        from_state(c, p, b, 0)
                        pe.wait_ge(s_sc, 16 * c + 4 * b + 2)
                    for g in (2 * pair, 2 * pair + 1):
                        for j in range(2):
                            for u in range(2):
                                rows, t0 = slice(32 * g, 32 * g + 32), b * P + HALF * u
                                col = (pair * 2 + j) * P
                                last = mm(ps_z[g % 2][HALF * u:HALF * u + HALF, col:col + P], kfT[rows, j, t0:t0 + HALF],
                                          qf[p][rows, :, t0:t0 + HALF], start=True, stop=True, skip_group_check=True)
                        last.then_inc(s_sc, 1)

            def from_state(c, p, b, u):
                t0 = b * P + HALF * u
                mm(ps_y[u][:, b * P:(b + 1) * P], state[p][:, b, u, :], qf[p][:, :, t0:t0 + HALF], start=(b == 0),
                   stop=False, skip_group_check=True)

            def outputs(c, p, b):
                pe.wait_ge(s_pr, 8 * c + 2 * b + 2)
                from_state(c, p, b, 1)
                cols = slice(b * P, (b + 1) * P)
                for j in range(2):
                    for u in range(2):
                        rows = slice(HALF * u, HALF * u + HALF)
                        for g in range(G):
                            col = (g // 2 * 2 + j) * P
                            last = mm(ps_y[u][32 * g:32 * g + 32, cols], v_pad[p][rows, j, b, g, :, :],
                                      probs[rows, b % 2, g % 2, col:col + P], start=False, stop=(j == 1),
                                      skip_group_check=True)
                last.then_inc(s_o, 1)

            def denominators(c):
                pe.wait_ge(s_prod, c + 1)
                if not first(c):
                    pe.wait_ge(s_y, 2 * c)
                for a in range(2):
                    last = mm(ps_w[0][32 * a:32 * a + 32, :], head_ones[:], prod[:, a, :], start=True, stop=True)
                last.then_inc(s_den_ps, 1)

            def denominators_by_token(c):
                pe.wait_ge(s_denT, c + 1)
                for b in range(NB):
                    last = tr(ps_w[1][:, b * P:(b + 1) * P], denT[:, b * P:(b + 1) * P], ident[:])
                last.then_inc(s_dtok_ps, 1)

            def reciprocals(c, mix):
                if mix:
                    pe.wait_ge(s_zT, 2 * c)
                pe.wait_ge(s_rden, c + 1)
                for b in range(NB):
                    last = tr(ps_w[0][0:32, b * P:(b + 1) * P], rden_parts[:, b, :, :], ident[:])
                last.then_inc(s_rT_ps, 1)

            def spread_reciprocals(c, last_chunk):
                if not last_chunk:
                    pe.wait_ge(s_kv, 5 * c + 7)
                pe.wait_ge(s_rT, c + 1)
                for a in range(2):
                    mm(ps_x[a][:, :], spread_r[0:32, a, :], rdenT[0:32, :], start=True, stop=True).then_inc(s_rb_ps, 1)

            def transpose_z(m, c):
                pe.wait_ge(s_z, 4 * m + 4)
                if c is not None:
                    pe.wait_ge(s_den, c + 1)
                for k in range(KD):
                    for b in range(NB):
                        last = tr(ps_w[k][:, b * P:(b + 1) * P], z_tok[:, b, k * P:(k + 1) * P], ident[:])
                    last.then_inc(s_zT_ps, 1)

            def mix_k(m, c):
                pe.wait_ge(s_xk, 2 * m + 2)
                if c is not None:
                    pe.wait_ge(s_rT, c + 1)
                for n in range(2):
                    for k in range(KD):
                        last = mm(ps_w[n][:, :], wkT[:, k, n * P:(n + 1) * P], xk[:, k, :, :], start=(k == 0),
                                  stop=(k == KD - 1))
                    last.then_inc(s_k_ps, 1)

            def mix_r(m, c):
                pe.wait_ge(s_xr, 2 * m + 2)
                if c is None:
                    pe.wait_ge(s_rb, 2 * m + 2)
                    pe.wait_ge(s_th, 2 * m)
                elif c == NC - 1 if isinstance(c, int) else False:
                    pe.wait_ge(s_rb, 2 * c + 2)
                else:
                    pe.wait_ge(s_ks, 4 * c + 8)
                for b in range(NB):
                    for k in range(KD):
                        last = mm(ps_x[b // 2][:, (b % 2) * D:(b % 2 + 1) * D], xr[:, k, b, :], wrT[:, k, :],
                                  start=(k == 0), stop=(k == KD - 1))
                    if b % 2:
                        last.then_inc(s_r_ps, 1)

            def mix_v(m):
                pe.wait_ge(s_ka, 2 * m + 2)
                for b in range(NB):
                    for k in range(KD):
                        last = mm(ps_w[b // 2][:, (b % 2) * D:(b % 2 + 1) * D], k_act[:, k, b * P:(b + 1) * P],
                                  wvT[:, k, :], start=(k == 0), stop=(k == KD - 1))
                    if b % 2:
                        last.then_inc(s_v_ps, 1)

            def step(c, p, mix, last):
                scores(c, p, 0)
                if mix:
                    out_projection(c - 1, 0)
                if not last:
                    transpose_a(c + 1)
                scores(c, p, 1)
                if mix:
                    out_projection(c - 1, 1)
                outputs(c, p, 0)
                denominators(c)
                scores(c, p, 2)
                if not last:
                    queries(c + 1, 0)
                outputs(c, p, 1)
                if not last:
                    queries(c + 1, 1)
                denominators_by_token(c)
                scores(c, p, 3)
                outputs(c, p, 2)
                if not last:
                    keys_values(c + 1)
                if mix:
                    transpose_z(c - 1, c)
                outputs(c, p, 3)
                reciprocals(c, mix)
                if not last:
                    state_increments(c + 1)
                spread_reciprocals(c, last)
                if not last:
                    key_sums(c + 1)
                if mix:
                    mix_k(c - 1, c)
                    mix_r(c - 1, c)
                    mix_v(c - 1)

            def mix_only(m, p):
                out_projection(m, 0)
                out_projection(m, 1)
                transpose_z(m, None)
                mix_k(m, None)
                mix_r(m, None)
                mix_v(m)

            transpose_a(0)
            queries(0, 0)
            queries(0, 1)
            keys_values(0)
            state_increments(0)
            key_sums(0)
            steps(pe, step, mix_only)

        @block.scalar
        def _(act):
            def copy(dst, src, **kw):
                return nc.scalar.activation(dst, src, ACT.Copy, **kw)

            act.wait_ge(prep_ps, 1)
            copy(wcT[0:64, :], ps_x[1][0:64, 0:64])
            copy(wkvT[0:64, :, :].rearrange("p i n -> p (i n)"), ps_x[0][0:64, :]).then_inc(prep_sb, 1)
            act.wait_ge(prep_ps, 2)
            copy(cewe[0:64, :], ps_x[1][0:64, 128:128 + KV]).then_inc(prep_sb, 1)
            copy(wrT[:].rearrange("p k n -> p (k n)"), ps_w[0][:, :])
            copy(wkT[:].rearrange("p k n -> p (k n)"), ps_w[1][:, :])
            copy(wvT[:].rearrange("p k n -> p (k n)"), ps_y[0][:, :], scale=0.5)
            act.wait_ge(prep_ps, 3)
            copy(wkv_sb[:].rearrange("p k n -> p (k n)"), ps_y[1][:, 0:256])
            copy(bkv_bc[:], ps_y[1][:, 256:384]).then_inc(prep_sb, 1)

            def a_out(n):
                for k in range(KD):
                    act.wait_ge(s_aT_ps, 2 * n + k + 1)
                    copy(aT[:, k, :], ps_x[k][:, :]).then_inc(s_aT, 1)

            def queries(n):
                for a in range(2):
                    act.wait_ge(s_q_ps, 2 * n + a + 1)
                    nc.scalar.activation(eq[:, a, :], ps_x[a][:, :], ACT.Relu, bias=neg_bq[:, a:a + 1],
                                         scale=-1.0).then_inc(s_nq, 1)
                for a in range(2):
                    act.wait_ge(s_nq, 2 * n + a + 1)
                    nc.scalar.activation(eq[:, a, :], eq[:, a, :], ACT.Exp, scale=-1.0).then_inc(s_eq, 1)

            def keys(n):
                act.wait_ge(s_kv, 5 * n + 1)
                nc.scalar.activation(ek[:], kb[:], ACT.Exp).then_inc(s_ek, 1)

            def key_sums(n):
                act.wait_ge(s_kT_ps, n + 1)
                for j in range(2):
                    copy(kfT[:, j, :], ps_x[0][:, :], scale=row_mask[:, j:j + 1]).then_inc(s_kT, 1)
                act.wait_ge(s_ks_ps, n + 1)
                if not first(n):
                    act.wait_ge(s_carry, n)
                for b in range(NB):
                    nc.scalar.activation(ksum[:, b * P:(b + 1) * P], ps_x[1][:, b * P:(b + 1) * P], ACT.Identity,
                                         bias=ksum_carry[:, b:b + 1]).then_inc(s_ks, 1)
                act.wait_ge(s_ks, 4 * n + 4)
                copy(ksum_carry[:], ksum[:].rearrange("p (b t) -> p b t", b=NB)[:, :, P - 1]).then_inc(s_carry, 1)

            def step(c, p, mix, last):
                if not last:
                    a_out(c + 1)
                act.wait_ge(s_den_ps, c + 1)
                copy(denT[0:64, :], ps_w[0][0:64, :]).then_inc(s_denT, 1)
                if not last:
                    queries(c + 1)
                if mix:
                    normalise_z(c - 1)
                if not last:
                    keys(c + 1)
                if mix:
                    shift_z(c - 1)
                act.wait_ge(s_rT_ps, c + 1)
                copy(rdenT[0:32, :], ps_w[0][0:32, :]).then_inc(s_rT, 1)
                for a in range(2):
                    act.wait_ge(s_rb_ps, 2 * c + a + 1)
                    copy(rden_bc[:, a, :], ps_x[a][:, :]).then_inc(s_rb, 1)
                if not last:
                    key_sums(c + 1)
                if mix:
                    channel(c - 1)

            def normalise_z(m):
                act.wait_ge(s_rs2, 2 * m + 2)
                act.wait_ge(s_nb, m + 1)
                for b in range(NB):
                    nc.scalar.activation(z_tok[:, b, :], x2_tok[:, b, :], ACT.Identity, bias=nbias2[:, b:b + 1],
                                         scale=rstd2[:, b:b + 1]).then_inc(s_z, 1)

            def shift_z(m):
                copy(zT[:, :, :, 0], zT[:, :, :, P]).then_inc(s_zcar, 1)
                act.wait_ge(s_zcar, m + 1)
                if not first(m):
                    act.wait_ge(s_xr, 2 * m)
                for k in range(KD):
                    act.wait_ge(s_zT_ps, 2 * m + k + 1)
                    copy(zT[:, k, :, 1:P + 1], ps_w[k][:, :].rearrange("p (b t) -> p b t", b=NB)).then_inc(s_zT, 1)

            def channel(m):
                for n in range(2):
                    act.wait_ge(s_k_ps, 2 * m + n + 1)
                    nc.scalar.activation(relu_k[:, n, :], ps_w[n][:, :], ACT.Relu).then_inc(s_rl, 1)
                for i in range(2):
                    act.wait_ge(s_r_ps, 2 * m + i + 1)
                    nc.scalar.activation(tanh_r[:, i, :], ps_x[i][:, :], ACT.Tanh, scale=0.5).then_inc(s_th, 1)

            def mix_only(m, p):
                normalise_z(m)
                shift_z(m)
                channel(m)

            act.wait_ge(dve_const, 1)
            a_out(0)
            queries(0)
            keys(0)
            key_sums(0)
            steps(act, step, mix_only)

        @block.vector
        def _(dve):
            V = nc.vector
            for t in (*v_pad, v_half, zT, ksum_carry, state[0], denT):
                V.memset(t[:], 0.0)
            V.memset(ones64[:], 1.0).then_inc(s_gt, 1)
            dve.wait_ge(pool_const, 1)
            dve.wait_ge(weights_in, 16 * WEIGHT_DMAS)
            for j in range(2):
                V.tensor_reduce(row_mask[:, j:j + 1], head_ones[:, j:8:2], AX_X, ALU.add)
            V.tensor_scalar(neg_bq[:], bq_col[:], -1.0, None, ALU.mult)
            V.tensor_copy(spread_r[0:32], spread[0:32])
            V.tensor_scalar(bq_1[:], bq_col[:], 1.0, None, ALU.add).then_inc(dve_const, 1)
            dve.wait_ge(dve_const, 1)
            for i in range(2):
                last = V.tensor_scalar(bkv_lhs[0:64, i, :], ones64[0:64, :], bkv_col[0:64, i:i + 1], None, ALU.mult)
            last.then_inc(bias_lhs, 1)

            def row_stats(src, stats, mv, done, c):
                for b in range(NB):
                    V.bn_stats(stats[:, b, :], src[:, b, :]).then_inc(done, 1)
                dve.wait_ge(done, 8 * c + NB)
                V.memset(wait_carrier[:], 0.0)
                for b in range(NB):
                    V.bn_aggr(mv[:, b, :], stats[:, b, :]).then_inc(done, 1)

            def norm_x(c, p):
                dve.wait_ge(x_loaded[p], 8 * c + (16 if p == 0 else 8))
                row_stats(x_in[p], stats0, mv0, s_st0, c)

            def norm_x_scale(c, p):
                dve.wait_ge(s_st0, 8 * c + 8)
                dve.wait_ge(s_rs0, 2 * c + 2)
                if not first(c):
                    dve.wait_ge(s_aT_ps, 2 * c)
                    dve.wait_ge(s_ab, c)
                for b in range(NB):
                    V.tensor_scalar(a_tok[:, b, :], x_in[p][:, b, :], mv0[:, b, 0:1], rstd0[:, b:b + 1], ALU.subtract,
                                    ALU.mult).then_inc(s_a, 1)

            def keys_values(n, p):
                dve.wait_ge(s_kv_ps, n + 1)
                kv = ps_x[0][:, :].rearrange("p (b n) -> p b n", b=NB)
                bias = bkv_bc[:].unsqueeze(1).to_broadcast([P, NB, 2 * KV])
                V.tensor_tensor(kb[:], kv[:, :, 0:KV], bias[:, :, 0:KV], ALU.add).then_inc(s_kv, 1)
                V.tensor_tensor(v_tok[:], kv[:, :, KV:2 * KV], bias[:, :, KV:2 * KV], ALU.add).then_inc(s_kv, 1)
                dve.wait_ge(s_kv, 5 * n + 2)
                V.tensor_copy(v_half[:, :, 1, :], v_tok[:])
                V.tensor_copy(v_half[0:HALF, :, 0, :], v_tok[0:HALF]).then_inc(s_kv, 1)
                for j in range(2):
                    V.tensor_copy(v_pad[p][:, j, :, :, j, :].rearrange("p b g d -> p (b g) d"),
                                  v_tok[:].rearrange("p b (g d) -> p (b g) d", d=HD)).then_inc(s_kv, 1)
                dve.wait_ge(s_ek, n + 1)
                V.tensor_scalar(ek[:], ek[:], 1.0, None, ALU.min).then_inc(s_ekm, 1)
                dve.wait_ge(s_ekm, n + 1)
                for j in range(2):
                    V.scalar_tensor_tensor(out=kf[:, :, j, :], in0=kb[:].rearrange("p b (g d) -> p (b g) d", d=HD),
                                           scalar=1.0, in1=ek[:].rearrange("p b (g d) -> p (b g) d", d=HD),
                                           op0=ALU.add, op1=ALU.max).then_inc(s_kf, 1)

            def queries(n, p):
                for a in range(2):
                    dve.wait_ge(s_eq, 2 * n + a + 1)
                    V.scalar_tensor_tensor(out=qf[p][:, a, :], in0=ps_x[a][:, :], scalar=bq_1[:, a:a + 1],
                                           in1=eq[:, a, :], op0=ALU.add, op1=ALU.max).then_inc(s_qf, 1)

            def add_residual(m, p, i):
                if i == 0:
                    dve.wait_ge(s_ab, m + 1)
                dve.wait_ge(s_y_ps, 2 * m + i + 1)
                V.tensor_tensor(y_tok[:, 2 * i:2 * i + 2, :], ps_w[i][:, :].rearrange("p (b d) -> p b d", b=2),
                                abo_tok[p][:, 2 * i:2 * i + 2, :], ALU.add).then_inc(s_y, 1)
                if i == 1:
                    dve.wait_ge(s_y, 2 * m + 2)
                    row_stats(y_tok, stats1, mv1, s_st1, m)

            def state_increment(c):
                dve.wait_ge(s_dS_ps, c + 1)
                if not first(c):
                    dve.wait_ge(s_next, c)
                V.tensor_tensor(dstate[:].rearrange("p b u (g j d) -> p (b u g) j d", g=G, j=2),
                                ps_z[1][:, :].rearrange("p (r d) -> p r d", d=HD).unsqueeze(2).to_broadcast([P, 32, 2, HD]),
                                head_rep[:].rearrange("p r (g j d) -> p (r g) j d", g=G, j=2),
                                ALU.mult).then_inc(s_dS, 1)

            def denominator_terms(c, p):
                dve.wait_ge(s_ks, 4 * c + 4)
                dve.wait_ge(s_qf, 2 * c + 2)
                V.tensor_tensor(prod[:], qf[p][:], ksum[:].unsqueeze(1).to_broadcast([P, 2, T]), ALU.mult).then_inc(s_prod, 1)

            def mask(c, b):
                if not (first(c) and b < 2):
                    dve.wait_ge(s_o, 4 * c + b - 1)
                for z in range(2):
                    dve.wait_ge(s_sc, 16 * c + 4 * b + z + 3)
                    V.tensor_tensor(probs[:, b % 2, z, :].rearrange("p (r s) -> p r s", s=HALF),
                                    ps_z[z][:, :].rearrange("p (r s) -> p r s", s=HALF),
                                    causal[:].unsqueeze(1).to_broadcast([P, 8, HALF]), ALU.mult).then_inc(s_pr, 1)

            def second_residual(m, p):
                dve.wait_ge(s_st1, 8 * m + 8)
                for b in range(NB):
                    V.scalar_tensor_tensor(out=t_tok[:, b, :], in0=y_tok[:, b, :], scalar=mv1[:, b, 0:1], in1=gamma_bc[:],
                                           op0=ALU.subtract, op1=ALU.mult).then_inc(s_t, 1)
                dve.wait_ge(s_rs1, 2 * m + 2)
                dve.wait_ge(s_xb, m + 1)
                dve.wait_ge(s_out, 2 * m + 1)
                for b in range(NB):
                    dve.wait_ge(s_t, 4 * m + b + 1)
                    V.scalar_tensor_tensor(out=x2_tok[:, b, :], in0=t_tok[:, b, :], scalar=rstd1[:, b:b + 1],
                                           in1=xb_tok[p][:, b, :], op0=ALU.mult, op1=ALU.add).then_inc(s_x2, 1)

            def second_stats(m):
                dve.wait_ge(s_x2, 4 * m + 4)
                row_stats(x2_tok, stats2, mv2, s_st2, m)

            def second_bias(m):
                dve.wait_ge(s_st2, 8 * m + 8)
                dve.wait_ge(s_rs2, 2 * m + 2)
                V.scalar_tensor_tensor(out=nbias2[:], in0=mv2[:, :, 0], scalar=-1.0, in1=rstd2[:], op0=ALU.mult,
                                       op1=ALU.mult).then_inc(s_nb, 1)

            def reciprocal(c):
                dve.wait_ge(s_dtok_ps, c + 1)
                V.tensor_scalar(den[:].rearrange("p b (a n) -> p b a n", a=2),
                                ps_w[1][:, :].rearrange("p (b a n) -> p b a n", b=NB, a=4)[:, :, 0:2, 0:8],
                                DEN_EPS, None, ALU.add).then_inc(s_den, 1)
                dve.wait_ge(s_den, c + 1)
                V.reciprocal(rden[:], den[:]).then_inc(s_rparts, 1)
                dve.wait_ge(s_rparts, 2 * c + 1)
                V.tensor_copy(rden_parts[:, :, 0, :].bitcast(F32R), rden[:]).then_inc(s_rparts, 1)
                dve.wait_ge(s_rparts, 2 * c + 2)
                V.tensor_tensor(rden_parts[:, :, 1, :], rden[:], rden_parts[:, :, 0, :], ALU.subtract).then_inc(s_rden, 1)

            def divide(c):
                dve.wait_ge(s_o, 4 * c + 4)
                dve.wait_ge(s_rb, 2 * c + 2)
                for u in range(2):
                    V.tensor_tensor(oT[:, :, :, u, :], ps_y[u][:, :].rearrange("p (b a s) -> p a b s", b=NB, a=2),
                                    rden_bc[:].rearrange("p a (b u s) -> p a b u s", b=NB, u=2)[:, :, :, u, :],
                                    ALU.mult).then_inc(s_oT, 1)

            def token_difference(m):
                dve.wait_ge(s_zT, 2 * m + 2)
                now, before = zT[:, :, :, 1:P + 1], zT[:, :, :, 0:P]
                V.tensor_tensor(dz[:], now.rearrange("p k b t -> p (k b) t"), before.rearrange("p k b t -> p (k b) t"),
                                ALU.subtract).then_inc(s_dz, 1)

            def token_shift(m):
                dve.wait_ge(s_dz, m + 1)
                for dst, mu, done in ((xk, mu_k_col, s_xk), (xr, mu_r_col, s_xr)):
                    for k in range(KD):
                        V.scalar_tensor_tensor(out=dst[:, k], in0=dz[:, k * NB:(k + 1) * NB, :], scalar=mu[:, k:k + 1],
                                               in1=zT[:, k, :, 0:P], op0=ALU.mult, op1=ALU.add).then_inc(done, 1)

            def square_k(m):
                for i in range(2):
                    dve.wait_ge(s_rl, 2 * m + i + 1)
                    V.tensor_tensor(k_act[:, i], relu_k[:, i], relu_k[:, i], ALU.mult).then_inc(s_ka, 1)

            def gate(m):
                for i in range(2):
                    dve.wait_ge(s_th, 2 * m + i + 1)
                    dve.wait_ge(s_v_ps, 2 * m + i + 1)
                    V.scalar_tensor_tensor(out=gated[:, i, :], in0=tanh_r[:, i, :], scalar=1.0, in1=ps_w[i][:, :],
                                           op0=ALU.add, op1=ALU.mult).then_inc(s_gt, 1)

            def step(c, p, mix, last):
                denominator_terms(c, p)
                mask(c, 0)
                if mix:
                    add_residual(c - 1, 1 - p, 0)
                mask(c, 1)
                if mix:
                    add_residual(c - 1, 1 - p, 1)
                if mix:
                    second_residual(c - 1, 1 - p)
                    second_stats(c - 1)
                mask(c, 2)
                if mix:
                    second_bias(c - 1)
                reciprocal(c)
                if not last:
                    queries(c + 1, 1 - p)
                mask(c, 3)
                if not last:
                    keys_values(c + 1, 1 - p)
                if mix:
                    token_difference(c - 1)
                    token_shift(c - 1)
                divide(c)
                if not last:
                    state_increment(c + 1)
                if within(c + 2):
                    norm_x(c + 2, p)
                if mix:
                    square_k(c - 1)
                if within(c + 2):
                    norm_x_scale(c + 2, p)
                if mix:
                    gate(c - 1)

            def mix_only(m, p):
                add_residual(m, p, 0)
                add_residual(m, p, 1)
                second_residual(m, p)
                second_stats(m)
                second_bias(m)
                token_difference(m)
                token_shift(m)
                square_k(m)
                gate(m)

            norm_x(0, 0)
            norm_x_scale(0, 0)
            dve.wait_ge(prep_sb, 3)
            norm_x(1, 1)
            queries(0, 0)
            norm_x_scale(1, 1)
            keys_values(0, 0)
            state_increment(0)
            steps(dve, step, mix_only)


_INS = ['L0_attn_x', 'L0_attn_Wq', 'L0_attn_bq', 'L0_attn_Wk', 'L0_attn_bk', 'L0_attn_Wv', 'L0_attn_bv', 'L0_attn_Wc',
        'L0_attn_We', 'L0_attn_Wo', 'L0_attn_bo', 'L0_attn_gamma', 'L0_attn_beta', 'L0_ffn_W_r', 'L0_ffn_W_k',
        'L0_ffn_W_v', 'L0_ffn_mu_r', 'L0_ffn_mu_k']


def kernel(**inputs):
    import numpy as _np
    import concourse.bacc as _bacc
    from concourse import mybir as _mybir
    from concourse.bass_utils import run_bass_kernel_spmd as _run

    nc = _bacc.Bacc("TRN2", target_bir_lowering=False, num_devices=1)
    arrays, args = {}, []
    for name in _INS:
        a = _np.ascontiguousarray(inputs[name])
        arrays[f"in_{name}_dram"] = a
        args.append(nc.dram_tensor(f"in_{name}_dram", a.shape, _mybir.dt.from_np(a.dtype), kind="ExternalInput").ap())
    args.append(nc.dram_tensor("out_dram", inputs['L0_attn_x'].shape, _mybir.dt.float32, kind="ExternalOutput").ap())
    build(nc, *args)
    r = _run(nc, [arrays], core_ids=[0])
    return r.results[0]["out_dram"]
```

```python
from contextlib import ExitStack

import numpy as np

import concourse.bass as bass
from concourse import mybir

P = 128
ALU = mybir.AluOpType
ACT = mybir.ActivationFunctionType
F32 = mybir.dt.float32
F32R = mybir.dt.float32r
AX_X = mybir.AxisListType.X

LN_EPS = 1e-5
DEN_EPS = 1e-6


def build(nc, x, wq, bq, wk, bk, wv, bv, wc, we, wo, bo, gamma, beta, w_r, w_k, w_v, mu_r, mu_k, out):
    NB, S, D = x.shape
    NC = S // P
    KD = D // P
    G, HD = 4, 16
    KV = G * HD
    HALF = P // 2
    T = NB * P
    assert D == 256 and NB == 4 and KV == wk.shape[1] and NC % 2 == 0

    def chunk_at(dram, start):
        return dram.rearrange("b t d -> b (t d)")[:, bass.ds(start, P * D)].rearrange("b (t d) -> t b d", d=D)

    with ExitStack() as ctx:
        def sb(name, *shape):
            return ctx.enter_context(nc.sbuf_tensor(name, [P, *shape], F32))

        def parts(name, *shape):
            return [ctx.enter_context(nc.sbuf_tensor(f"{name}_{part}", [P, *shape], F32R)) for part in ("high", "low")]

        def sem(name):
            return ctx.enter_context(nc.semaphore(name))

        def bank(name):
            return ctx.enter_context(nc.psum_tensor(name, [P, 512], F32))

        ps_x = [bank("ps_x0"), bank("ps_x1")]
        ps_y = [bank("ps_y0"), bank("ps_y1")]
        ps_z = [bank("ps_z0"), bank("ps_z1")]
        ps_w = [bank("ps_w0"), bank("ps_w1")]
        ffn_banks = (ps_w[0], ps_y[1], ps_x[0])

        ident = sb("ident", P)
        tri = sb("tri", P)
        causal = sb("causal", HALF)
        head_ones = sb("head_ones", 32)
        head_rep = sb("head_rep", 2 * NB, P)
        spread_r = ctx.enter_context(nc.sbuf_tensor("spread_r", [P, 2, P], F32R))
        row_mask = sb("row_mask", 2)
        neg_one, nbias0, neg_mean0, neg_mean2 = sb("neg_one", NB), sb("nbias0", NB), sb("neg_mean0", NB), sb("neg_mean2", NB)
        neg_half, ln_eps = sb("neg_half", NB), sb("ln_eps", NB)
        ones64, wait_carrier = sb("ones64", P), sb("wait_carrier", 1)

        wc_in, we_in = sb("wc_in", 64), sb("we_in", 64)
        bkv_col = sb("bkv_col", 2)
        wo_sb = sb("wo_sb", 2, D)
        bq_col, neg_bq, bq_1 = sb("bq_col", 2), sb("neg_bq", 2), sb("bq_1", 2)
        gamma_bc, beta_bc, bo_bc = sb("gamma_bc", D), sb("beta_bc", D), sb("bo_bc", D)
        mu_r_col, mu_k_col = sb("mu_r_col", KD), sb("mu_k_col", KD)
        wcT, cewe = sb("wcT", 64), sb("cewe", KV)
        wkv_sb, bkv_bc = sb("wkv_sb", KD, 2 * KV), sb("bkv_bc", 2 * KV)

        x_in = [sb(f"x_in{i}", NB, D) for i in range(2)]
        a_tok = sb("a_tok", NB, D)
        abo_tok = [sb(f"abo_tok{i}", NB, D) for i in range(2)]
        xb_tok = [sb(f"xb_tok{i}", NB, D) for i in range(2)]
        stats0, mv0, rstd0 = sb("stats0", NB, 6), sb("mv0", NB, 2), sb("rstd0", NB)
        aT = sb("aT", KD, T)
        qf = [sb(f"qf{i}", 2, T) for i in range(2)]
        kb, ek = sb("kb", NB, KV), sb("ek", NB, KV)
        v_pad = [sb(f"v_pad{i}", NB, 2, G, 2, HD) for i in range(2)]
        v_half = sb("v_half", NB, 2, KV)
        kf = sb("kf", NB * G, 2, HD)
        kfT = sb("kfT", 2 * NB, 2, HALF)
        ksum, ksum_carry = sb("ksum", T), sb("ksum_carry", NB)
        prod = sb("prod", 2, T)
        denT, den, rden, rdenT, rden_bc = sb("denT", T), sb("den", NB, 16), sb("rden", NB, 16), ctx.enter_context(nc.sbuf_tensor("rdenT", [P, T], F32R)), sb("rden_bc", 2, T)
        rden_parts = sb("rden_parts", NB, 2, 16)
        dstate = sb("dstate", NB, 2, P)
        state = [sb(f"state{i}", NB, 2, P) for i in range(2)]
        probs = sb("probs", 2, 2, 512)
        y_tok, t_tok, z_tok = sb("y_tok", NB, D), sb("t_tok", NB, D), sb("z_tok", NB, D)
        x2_tok = [sb(f"x2_tok{i}", NB, D) for i in range(2)]
        stats1, mv1, rstd1 = sb("stats1", NB, 6), sb("mv1", NB, 2), sb("rstd1", NB)
        stats2, mv2, rstd2, nbias2 = sb("stats2", NB, 6), sb("mv2", NB, 2), sb("rstd2", NB), sb("nbias2", NB)
        zT = sb("zT", KD, NB, P + 1)
        relu_k, k_act = sb("relu_k", 2, T), sb("k_act", T)
        tanh_r, out_tok = sb("tanh_r", 2, 512), sb("out_tok", NB, D)

        def flat(t):
            names = "abcd"[:len(t.shape) - 1]
            return t[:] if len(names) == 1 else t[:].rearrange(f"p {' '.join(names)} -> p ({' '.join(names)})")

        def view(t, start, *shape):
            part = flat(t)[:, start:start + int(np.prod(shape))]
            names = "abcd"[:len(shape)]
            return part.rearrange(f"p ({' '.join(names)}) -> p {' '.join(names)}", **dict(zip(names, shape)))

        eq = view(prod, 0, 2, T)
        oT = view(probs, 2 * 512, 2, NB, 2, HALF)
        dz, xk, xr = view(t_tok, 0, KD * NB, P), view(y_tok, 0, KD, NB, P), view(z_tok, 0, KD, NB, P)
        gated = tanh_r
        ffn_in = [view(relu_k, 0, KD, D), view(relu_k, KD * D, KD, D), view(tanh_r, 0, KD, D)]
        wq_in = view(tanh_r, KD * D, KD, D)
        wkvT, bkv_lhs = view(rden_bc, 0, 2, D), view(rden_bc, 2 * D, 2, P)
        wk_in, wv_in = view(rden_bc, 2 * D + 2 * P, KD, KV), view(rden_bc, 2 * D + 2 * P + KD * KV, KD, KV)
        spread = view(y_tok, 0, 2, P)

        wq_p, wo_p = parts("wq", KD, 2, P), parts("wo", 2, D)
        wr_p, wk_p, wv_p = parts("wrT", KD, D), parts("wkT", KD, D), parts("wvT", KD, D)
        aT_p, oT_p = parts("aT", KD, T), parts("oT", 2, NB, 2, HALF)
        xr_p, xk_p, ka_p = parts("xr", KD, NB, P), parts("xk", KD, NB, P), parts("k_act", 2, T)

        kv_in, q_in, ffn_w_in, rows_in = sem("kv_weights_in"), sem("q_weights_in"), sem("ffn_weights_in"), sem("rows_in")
        wq_ready, out_stored = sem("wq_ready"), sem("out_stored")
        x_loaded = [sem("x_loaded0"), sem("x_loaded1")]
        pool_const, dve_const, prep_ps, prep_sb = sem("pool_const"), sem("dve_const"), sem("prep_ps"), sem("prep_sb")
        pool_link, bias_lhs = sem("pool_link"), sem("bias_lhs")
        s_st0, s_rs0, s_a, s_xb, s_ab = sem("stats0_done"), sem("rstd0_done"), sem("a_ready"), sem("xbeta_ready"), sem("abo_ready")
        s_aT_ps, s_aT = sem("aT_ps"), sem("aT_ready")
        s_q_ps, s_nq, s_eq, s_qf = sem("q_ps"), sem("negq"), sem("expq"), sem("qf_ready")
        s_kv_ps, s_kv, s_ek, s_ekm, s_kf = sem("kv_ps"), sem("kv_ready"), sem("expk"), sem("expk_min"), sem("kf_ready")
        s_kT_ps, s_kT, s_ks_ps, s_ks, s_carry = sem("kT_ps"), sem("kT_ready"), sem("ksum_ps"), sem("ksum_ready"), sem("carry_ready")
        s_dS_ps, s_dS, s_mid, s_next = sem("dstate_ps"), sem("dstate_ready"), sem("state_mid"), sem("state_next")
        s_prod, s_den_ps, s_denT, s_dtok_ps, s_den, s_rden = (
            sem("prod_ready"), sem("den_ps"), sem("denT_ready"), sem("dtok_ps"), sem("den_ready"), sem("rden_ready"))
        s_rparts = sem("rden_high_ready")
        s_aTh, s_aTl, s_oTh, s_oTl = sem("aT_high"), sem("aT_low"), sem("oT_high"), sem("oT_low")
        s_xkh, s_xkl, s_xrh, s_xrl, s_kah, s_kal = (
            sem("xk_high"), sem("xk_low"), sem("xr_high"), sem("xr_low"), sem("kact_high"), sem("kact_low"))
        s_nb0, s_vh, s_vp = sem("nbias0_ready"), sem("v_half_ready"), sem("v_heads_ready")
        wo_high, wo_low, weights_low = sem("wo_high"), sem("wo_low"), sem("weights_low")
        s_rT_ps, s_rT, s_rb_ps, s_rb = sem("rdenT_ps"), sem("rdenT_ready"), sem("rdenbc_ps"), sem("rdenbc_ready")
        s_sc, s_pr, s_o, s_oT = sem("scores_ps"), sem("probs_ready"), sem("o_ps"), sem("oT_ready")
        s_y_ps, s_y, s_st1, s_rs1, s_t, s_x2 = (
            sem("y_ps"), sem("y_ready"), sem("stats1_done"), sem("rstd1_done"), sem("t_ready"), sem("x2_ready"))
        s_st2, s_rs2, s_nb, s_z = sem("stats2_done"), sem("rstd2_done"), sem("nbias2_ready"), sem("z_ready")
        s_zT_ps, s_zcar, s_zT, s_dz, s_xk, s_xr = (
            sem("zT_ps"), sem("zshift_ready"), sem("zT_ready"), sem("dz_ready"), sem("xk_ready"), sem("xr_ready"))
        s_k_ps, s_rl, s_ka, s_r_ps, s_th, s_v_ps, s_gt, s_out = (
            sem("k_ps"), sem("relu_ready"), sem("kact_ready"), sem("r_ps"), sem("tanh_ready"), sem("v_ps"),
            sem("gated_ready"), sem("out_ready"))

        first = lambda c: isinstance(c, int) and c == 0
        within = lambda c: not isinstance(c, int) or c < NC

        def steps(eng, step, finale):
            step(0, 0, False)
            step(1, 1, True)
            with eng.Fori(0, NC // 2 - 2) as pair:
                step(2 * pair + 2, 0, True)
                step(2 * pair + 3, 1, True)
            step(NC - 2, 0, True)
            finale(NC - 1, 1)

        block = ctx.enter_context(nc.Block())

        kv_loads = [(wk_in[:], wk.rearrange("(k p) n -> p k n", p=P)), (wv_in[:], wv.rearrange("(k p) n -> p k n", p=P)),
                    (wc_in[0:64, :], wc), (we_in[0:64, :], we),
                    (bkv_col[0:64, 0:1], bk.rearrange("(n o) -> n o", o=1)),
                    (bkv_col[0:64, 1:2], bv.rearrange("(n o) -> n o", o=1))]
        q_loads = [(wq_in[:], wq.rearrange("(k p) n -> p k n", p=P))]
        q_loads += [(bq_col[32 * g:32 * g + 32, :], bq[64 * g:64 * g + 64].rearrange("(a m) -> m a", a=2)) for g in range(G)]
        ffn_loads = [(dst[:], w.rearrange("(k p) n -> p k n", p=P))
                     for w, dst in ((w_r, ffn_in[0]), (w_k, ffn_in[1]), (w_v, ffn_in[2]))]
        row_loads = [(dst[:], v.partition_broadcast(P)) for v, dst in ((bo, bo_bc), (beta, beta_bc), (gamma, gamma_bc))]
        row_loads += [(wo_sb[32 * g:32 * g + 32, :, :], wo[64 * g:64 * g + 64, :].rearrange("(a m) n -> m a n", a=2))
                      for g in range(G)]
        row_loads += [(dst[:], v.rearrange("(k p) -> p k", p=P)) for v, dst in ((mu_r, mu_r_col), (mu_k, mu_k_col))]
        KV_IN, Q_IN, FFN_IN, ROWS_IN = (16 * len(part) for part in (kv_loads, q_loads, ffn_loads, row_loads))

        @block.sync
        def _(sp):
            sp.sem_inc(out_stored, 16)
            def load(n, p):
                sp.dma_start(x_in[p][:], chunk_at(x, n * P * D)).then_inc(x_loaded[p], 16)

            def load_ahead(c, p):
                sp.wait_ge(s_xb, c + 1)
                sp.wait_ge(s_a, 4 * c + 4)
                load(c + 2, p)

            def store(m):
                sp.wait_ge(s_out, 2 * m + 3)
                sp.dma_start(chunk_at(out, m * P * D), out_tok[:]).then_inc(out_stored, 16)

            load(0, 0)
            with nc.allow_non_contiguous_dma(reason="bias and mixing vectors, one element a partition"):
                for dst, src in kv_loads:
                    sp.dma_start(dst, src).then_inc(kv_in, 16)
                load(1, 1)
                for dst, src in ffn_loads:
                    sp.dma_start(dst, src).then_inc(ffn_w_in, 16)
                for dst, src in row_loads:
                    sp.dma_start(dst, src).then_inc(rows_in, 16)
            load_ahead(0, 0)
            with sp.Fori(0, NC // 2 - 2) as pair:
                for i, p in ((1, 1), (2, 0)):
                    load_ahead(2 * pair + i, p)
                    store(2 * pair + i - 1)
            load_ahead(NC - 3, 1)
            for m in range(NC - 4, NC - 1):
                store(m)
            for i in range(2):
                sp.wait_ge(s_out, 2 * NC + i)
                sp.dma_start(chunk_at(out, (NC - 1) * P * D)[:, 2 * i:2 * i + 2, :],
                             out_tok[:, 2 * i:2 * i + 2, :]).then_inc(out_stored, 16)
            sp.wait_ge(out_stored, 16 * NC + 32)

        @block.gpsimd
        def _(pool):
            links = [0]

            def link(ins):
                links[0] += 1
                ins.then_inc(pool_link, 1)
                pool.wait_ge(pool_link, links[0])

            def rstd(dst, mv, eps, stats_done, stats_value, done, value):
                pool.wait_ge(stats_done, stats_value)
                nc.gpsimd.tensor_tensor(dst[:], mv[:, :, 1], eps[:], ALU.add).then_inc(done, 1)
                pool.wait_ge(done, value)
                nc.gpsimd.tensor_tensor(dst[:], dst[:], neg_half[:], ALU.pow).then_inc(done, 1)

            def scale_and_bias(dst, neg_mean, nbias, mv, stats_done, done, bias_done, n):
                pool.wait_ge(stats_done, 8 * n + 8)
                nc.gpsimd.tensor_tensor(neg_mean[:], mv[:, :, 0], neg_one[:], ALU.mult).then_inc(bias_done, 1)
                rstd(dst, mv, ln_eps, stats_done, 8 * n + 8, done, 2 * n + 1)
                pool.wait_ge(done, 2 * n + 2)
                pool.wait_ge(bias_done, 2 * n + 1)
                nc.gpsimd.tensor_tensor(nbias[:], neg_mean[:], dst[:], ALU.mult).then_inc(bias_done, 1)

            def norm_x(n):
                scale_and_bias(rstd0, neg_mean0, nbias0, mv0, s_st0, s_rs0, s_nb0, n)

            def add_beta(n, p):
                if not isinstance(n, int) or n >= 2:
                    pool.wait_ge(s_x2, 4 * n - 4)
                nc.gpsimd.tensor_tensor(xb_tok[p][:], x_in[p][:], beta_bc[:].unsqueeze(1).to_broadcast([P, NB, D]),
                                        ALU.add).then_inc(s_xb, 1)

            def split_a(n):
                pool.wait_ge(s_aTh, 2 * n + 2)
                nc.gpsimd.tensor_tensor(aT_p[1][:], aT[:], aT_p[0][:].bitcast(F32), ALU.subtract).then_inc(s_aTl, 1)

            def split_o(c):
                pool.wait_ge(s_oTh, c + 1)
                for a in range(2):
                    nc.gpsimd.tensor_tensor(oT_p[1][:, a], oT[:, a], oT_p[0][:, a].bitcast(F32), ALU.subtract).then_inc(s_oTl, 1)

            def add_bo(c, p):
                pool.wait_ge(s_a, 4 * c + 4)
                if not isinstance(c, int) or c >= 2:
                    pool.wait_ge(s_y, 2 * c - 2)
                nc.gpsimd.tensor_tensor(abo_tok[p][:], a_tok[:], bo_bc[:].unsqueeze(1).to_broadcast([P, NB, D]),
                                        ALU.add).then_inc(s_ab, 1)

            def first_norm(m):
                rstd(rstd1, mv1, ln_eps, s_st1, 8 * m + 8, s_rs1, 2 * m + 1)

            def second_norm(m):
                scale_and_bias(rstd2, neg_mean2, nbias2, mv2, s_st2, s_rs2, s_nb, m)

            def denominator_terms(c, p):
                pool.wait_ge(s_ks, 4 * c + 4)
                pool.wait_ge(s_qf, 2 * c + 2)
                nc.gpsimd.tensor_tensor(prod[:], qf[p][:], ksum[:].unsqueeze(1).to_broadcast([P, 2, T]),
                                        ALU.mult).then_inc(s_prod, 1)

            def finish(m, p):
                pool.wait_ge(out_stored, 16 * m + 16)
                for i in range(2):
                    pool.wait_ge(s_gt, 2 * m + i + 2)
                    nc.gpsimd.tensor_tensor(out_tok[:, 2 * i:2 * i + 2, :],
                                            gated[:, i].rearrange("p (b d) -> p b d", b=2),
                                            x2_tok[p][:, 2 * i:2 * i + 2, :], ALU.add).then_inc(s_out, 1)

            def token_difference(m):
                for k in range(KD):
                    pool.wait_ge(s_zT, 2 * m + k + 1)
                    nc.gpsimd.tensor_tensor(dz[:, k * NB:(k + 1) * NB, :], zT[:, k, :, 1:P + 1], zT[:, k, :, 0:P],
                                            ALU.subtract).then_inc(s_dz, 1)

            def next_state(n, p):
                pool.wait_ge(s_dS, n + 1)
                if not first(n):
                    pool.wait_ge(s_next, n)
                nc.gpsimd.tensor_tensor(state[1 - p][:, :, 0, :], state[p][:, :, 0, :], dstate[:, :, 1, :],
                                        ALU.add).then_inc(s_next, 1)

            def step(c, p, mix):
                if mix:
                    first_norm(c - 1)
                split_a(c + 1)
                if mix:
                    second_norm(c - 1)
                add_bo(c + 1, 1 - p)
                add_beta(c + 1, 1 - p)
                if mix:
                    token_difference(c - 1)
                denominator_terms(c + 1, 1 - p)
                if mix:
                    split_o(c)
                next_state(c + 1, 1 - p)
                if within(c + 2):
                    norm_x(c + 2)
                if mix:
                    finish(c - 1, 1 - p)

            def finale(c, p):
                first_norm(c - 1)
                second_norm(c - 1)
                token_difference(c - 1)
                for k in range(KD):
                    pool.wait_ge(s_xrh, 2 * c + k - 1)
                    nc.gpsimd.tensor_tensor(xr_p[1][:, k], xr[:, k], xr_p[0][:, k].bitcast(F32),
                                            ALU.subtract).then_inc(s_xrl, 1)
                first_norm(c)
                for i in range(2):
                    pool.wait_ge(s_ka, 2 * c + i - 1)
                    pool.wait_ge(s_kah, 2 * c + i - 1)
                    nc.gpsimd.tensor_tensor(ka_p[1][:, i], k_act[:], ka_p[0][:, i].bitcast(F32),
                                            ALU.subtract).then_inc(s_kal, 1)
                second_norm(c)
                finish(c - 1, 1 - p)

            link(nc.gpsimd.memset(ident[:], 0.0))
            link(nc.gpsimd.affine_select(out=ident[:], in_=ident[:], compare_op=ALU.not_equal, fill=1.0, base=0,
                                         pattern=[[-1, P]], channel_multiplier=1))
            link(nc.gpsimd.memset(head_ones[:], 1.0))
            link(nc.gpsimd.affine_select(out=head_ones[:], in_=head_ones[:], compare_op=ALU.is_ge, fill=0.0, base=0,
                                         pattern=[[-16, 32]], channel_multiplier=1))
            link(nc.gpsimd.affine_select(out=head_ones[:], in_=head_ones[:], compare_op=ALU.is_ge, fill=0.0, base=15,
                                         pattern=[[16, 32]], channel_multiplier=-1))
            link(nc.gpsimd.memset(ln_eps[:], LN_EPS))
            link(nc.gpsimd.memset(neg_one[:], -1.0))
            nc.gpsimd.memset(neg_half[:], -0.5).then_inc(pool_const, 1)
            pool.wait_ge(pool_const, 1)
            for t in (zT, state[0], denT):
                nc.gpsimd.memset(t[:], 0.0)
            norm_x(0)
            link(nc.gpsimd.memset(tri[:], 1.0))
            link(nc.gpsimd.affine_select(out=tri[:], in_=tri[:], compare_op=ALU.is_ge, fill=0.0, base=0,
                                         pattern=[[1, P]], channel_multiplier=-1))
            link(nc.gpsimd.memset(causal[:], 1.0))
            for u in range(2):
                half = causal[HALF * u:HALF * u + HALF, :]
                link(nc.gpsimd.affine_select(out=half, in_=half, compare_op=ALU.is_ge, fill=0.0, base=0,
                                             pattern=[[1, HALF]], channel_multiplier=-1))
            link(nc.gpsimd.memset(head_rep[:], 1.0))
            rep = head_rep[:].rearrange("p r (n d) -> p r n d", d=HD)
            link(nc.gpsimd.affine_select(out=rep, in_=rep, compare_op=ALU.is_ge, fill=0.0, base=0,
                                         pattern=[[0, 2 * NB], [-16, 8], [0, HD]], channel_multiplier=1))
            link(nc.gpsimd.affine_select(out=rep, in_=rep, compare_op=ALU.is_ge, fill=0.0, base=15,
                                         pattern=[[0, 2 * NB], [16, 8], [0, HD]], channel_multiplier=-1))
            link(nc.gpsimd.memset(spread[:], 0.0))
            spr = spread[0:32, :, :].rearrange("p a (n d) -> p a n d", d=HD)
            for part in range(2):
                last = nc.gpsimd.affine_select(out=spr, in_=spr, compare_op=ALU.not_equal, fill=1.0, base=-16 * part,
                                               pattern=[[-8, 2], [-1, 8], [0, HD]], channel_multiplier=1)
                if part == 0:
                    link(last)
            last.then_inc(pool_const, 1)
            nc.gpsimd.memset(out_tok[:, 0, 0:1], 0.0).then_inc(s_out, 1)
            norm_x(1)
            pool.wait_ge(rows_in, ROWS_IN)
            add_bo(0, 0)
            add_beta(0, 0)
            denominator_terms(0, 0)
            next_state(0, 0)
            pool.wait_ge(wo_high, 1)
            nc.gpsimd.tensor_tensor(wo_p[1][:], wo_sb[:], wo_p[0][:].bitcast(F32), ALU.subtract).then_inc(wo_low, 1)
            steps(pool, step, finale)

        @block.tensor
        def _(pe):
            mm, tr = nc.tensor.matmul, nc.tensor.transpose
            def product(out, lhs, rhs, first_k, last_k):
                mm(out, lhs[0], rhs[0], start=first_k, stop=False)
                mm(out, lhs[0], rhs[1], start=False, stop=False)
                return mm(out, lhs[1], rhs[0], start=False, stop=last_k)

            def transpose_a(n):
                pe.wait_ge(s_a, 4 * n + 4)
                if not first(n):
                    pe.wait_ge(s_ks, 4 * n)
                for k in range(KD):
                    for b in range(NB):
                        last = tr(ps_x[k][:, b * P:(b + 1) * P], a_tok[:, b, k * P:(k + 1) * P], ident[:])
                    last.then_inc(s_aT_ps, 1)

            def queries(n, a):
                if a == 0:
                    pe.wait_ge(s_aTl, n + 1)
                for k in range(KD):
                    last = product(ps_x[a][:, :], [w[:, k, a, :] for w in wq_p], [t[:, k, :] for t in aT_p],
                                   k == 0, k == KD - 1)
                last.then_inc(s_q_ps, 1)

            def keys_values(n, bank):
                for b in range(NB):
                    for k in range(KD):
                        last = mm(bank[:, b * P:(b + 1) * P], aT[:, k, b * P:(b + 1) * P], wkv_sb[:, k, :],
                                  start=(k == 0), stop=(k == KD - 1))
                last.then_inc(s_kv_ps, 1)

            def out_projection(m, i, banks):
                if i == 0:
                    pe.wait_ge(s_oTl, 2 * m + 2)
                if banks is ps_w:
                    pe.wait_ge(s_gt, 2 * m + 1)
                for b in (2 * i, 2 * i + 1):
                    for a in range(2):
                        last = product(banks[i][:, (b % 2) * D:(b % 2 + 1) * D], [t[:, a, b, :, :] for t in oT_p],
                                       [w[:, a, :] for w in wo_p], a == 0, a == 1)
                last.then_inc(s_y_ps, 1)

            def key_sums(n, banks):
                pe.wait_ge(s_kf, 2 * n + 2)
                if not first(n):
                    pe.wait_ge(s_rb, 2 * n)
                for b in range(NB):
                    last = tr(banks[0][:, b * P:(b + 1) * P], kf[:, b * G:(b + 1) * G, :, :], ident[:])
                last.then_inc(s_kT_ps, 1)
                for b in range(NB):
                    last = mm(banks[1][:, b * P:(b + 1) * P], kf[:, b * G:(b + 1) * G, :, :], tri[:], start=True, stop=True)
                last.then_inc(s_ks_ps, 1)

            def state_increments(n):
                pe.wait_ge(s_kf, 2 * n + 2)
                pe.wait_ge(s_kv, 2 * n + 2)
                pe.wait_ge(s_vh, n + 1)
                if not first(n):
                    pe.wait_ge(s_pr, 8 * n)
                for b in range(NB):
                    last = mm(ps_z[1][:, b * P:(b + 1) * P], kf[:, b * G:(b + 1) * G, :, :], v_half[:, b, :, :],
                              start=True, stop=True)
                last.then_inc(s_dS_ps, 1)

            def scores(c, p, b):
                if b == 0:
                    pe.wait_ge(s_kT, 2 * c + 2)
                    pe.wait_ge(s_dS, c + 1)
                    if not first(c):
                        pe.wait_ge(s_oT, 2 * c)
                else:
                    pe.wait_ge(s_pr, 8 * c + 2 * b)
                for pair in range(2):
                    if pair:
                        if b == 0:
                            pe.wait_ge(s_mid, c + 1)
                        from_state(c, p, b, 0)
                        pe.wait_ge(s_sc, 16 * c + 4 * b + 2)
                    for g in (2 * pair, 2 * pair + 1):
                        for u in range(2):
                            rows, t0 = slice(32 * g, 32 * g + 32), b * P + HALF * u
                            col = (pair * 2 + u) * P
                            last = mm(ps_z[g % 2][:, col:col + P], kfT[rows, 2 * b + u, :, :], qf[p][rows, :, t0:t0 + HALF],
                                      start=True, stop=True, skip_group_check=True)
                        last.then_inc(s_sc, 1)

            def from_state(c, p, b, u):
                t0 = b * P + HALF * u
                mm(ps_y[u][:, b * P:(b + 1) * P], state[p][:, b, u, :], qf[p][:, :, t0:t0 + HALF], start=(b == 0),
                   stop=False, skip_group_check=True)

            def outputs(c, p, b):
                pe.wait_ge(s_pr, 8 * c + 2 * b + 2)
                if b == 0:
                    pe.wait_ge(s_vp, 4 * c + 4)
                from_state(c, p, b, 1)
                cols = slice(b * P, (b + 1) * P)
                for u in range(2):
                    for g in range(G):
                        col = (g // 2 * 2 + u) * P
                        last = mm(ps_y[u][32 * g:32 * g + 32, cols], v_pad[p][:, b, u, g, :, :],
                                  probs[:, b % 2, g % 2, col:col + P], start=False, stop=True, skip_group_check=True)
                last.then_inc(s_o, 1)

            def denominators(c, banks=ps_w):
                pe.wait_ge(s_prod, c + 1)
                if banks is ps_w and not first(c):
                    pe.wait_ge(s_y, 2 * c)
                for a in range(2):
                    last = mm(banks[0][32 * a:32 * a + 32, :], head_ones[:], prod[:, a, :], start=True, stop=True)
                last.then_inc(s_den_ps, 1)

            def denominators_by_token(c, banks=ps_w):
                pe.wait_ge(s_denT, c + 1)
                for b in range(NB):
                    last = tr(banks[1][:, b * P:(b + 1) * P], denT[:, b * P:(b + 1) * P], ident[:])
                last.then_inc(s_dtok_ps, 1)

            def reciprocals(c, mix, banks=ps_w):
                if mix:
                    pe.wait_ge(s_zT, 2 * c)
                pe.wait_ge(s_rden, c + 1)
                for b in range(NB):
                    last = tr(banks[0][0:32, b * P:(b + 1) * P], rden_parts[:, b, :, :], ident[:])
                last.then_inc(s_rT_ps, 1)

            def spread_reciprocals(c):
                if c != NC - 1 if isinstance(c, int) else True:
                    pe.wait_ge(s_kv, 2 * c + 4)
                pe.wait_ge(s_rT, c + 1)
                for a in range(2):
                    mm(ps_x[a][:, :], spread_r[0:32, a, :], rdenT[0:32, :], start=True, stop=True).then_inc(s_rb_ps, 1)

            def transpose_z(m, c, banks=ps_w):
                if banks is ps_z:
                    pe.wait_ge(s_y, 2 * m + 2)
                elif c is None:
                    pe.wait_ge(s_gt, 2 * m + 1)
                else:
                    pe.wait_ge(s_den, c + 1)
                for b in range(NB):
                    pe.wait_ge(s_z, 4 * m + b + 1)
                    for k in range(KD):
                        last = tr(banks[k][:, b * P:(b + 1) * P], z_tok[:, b, k * P:(k + 1) * P], ident[:])
                        if b == NB - 1:
                            last.then_inc(s_zT_ps, 1)

            def mix_k(m, c, banks=ps_w):
                if c is not None:
                    pe.wait_ge(s_rT, c + 1)
                for n in range(2):
                    for k in range(KD):
                        if n == 0:
                            pe.wait_ge(s_xkh, 2 * m + k + 1)
                        for part in range(2):
                            mm(banks[n][:, :], wk_p[part][:, k, n * P:(n + 1) * P], xk_p[0][:, k, :, :],
                               start=(k == 0 and part == 0), stop=False)
                    for k in range(KD):
                        if n == 0:
                            pe.wait_ge(s_xkl, 2 * m + k + 1)
                        last = mm(banks[n][:, :], wk_p[0][:, k, n * P:(n + 1) * P], xk_p[1][:, k, :, :],
                                  start=False, stop=(k == KD - 1))
                    last.then_inc(s_k_ps, 1)

            def high_then_low(out, x, w, low_ready, value):
                for k in range(KD):
                    for part in range(2):
                        mm(out, x[0][k], w[part][:, k, :], start=(k == 0 and part == 0), stop=False)
                for k in range(KD):
                    if low_ready is not None:
                        pe.wait_ge(low_ready, value + k + 1)
                    last = mm(out, x[1][k], w[0][:, k, :], start=False, stop=(k == KD - 1))
                return last

            def mix_r(m, c):
                pe.wait_ge(s_xrh, 2 * m + 2)
                if c is None:
                    pe.wait_ge(s_th, 2 * m)
                elif c == NC - 1 if isinstance(c, int) else False:
                    pe.wait_ge(s_rb, 2 * c + 2)
                else:
                    pe.wait_ge(s_ks, 4 * c + 8)
                for b in range(NB):
                    last = high_then_low(ps_x[b // 2][:, (b % 2) * D:(b % 2 + 1) * D],
                                         [[t[:, k, b, :] for k in range(KD)] for t in xr_p], wr_p,
                                         s_xrl if b == 0 else None, 2 * m)
                    if b % 2:
                        last.then_inc(s_r_ps, 1)

            def mix_v(m):
                pe.wait_ge(s_gt, 2 * m + 1)
                pe.wait_ge(s_kah, 2 * m + 2)
                for b in range(NB):
                    last = high_then_low(ps_w[b // 2][:, (b % 2) * D:(b % 2 + 1) * D],
                                         [[t[:, k, b * P:(b + 1) * P] for k in range(KD)] for t in ka_p], wv_p,
                                         s_kal if b == 0 else None, 2 * m)
                    if b % 2:
                        last.then_inc(s_v_ps, 1)

            def step(c, p, mix):
                scores(c, p, 0)
                if mix:
                    out_projection(c - 1, 0, ps_w)
                    out_projection(c - 1, 1, ps_w)
                scores(c, p, 1)
                if not mix:
                    pe.wait_ge(weights_low, 3)
                transpose_a(c + 1)
                outputs(c, p, 0)
                denominators(c)
                scores(c, p, 2)
                outputs(c, p, 1)
                queries(c + 1, 0)
                queries(c + 1, 1)
                denominators_by_token(c)
                scores(c, p, 3)
                if mix:
                    transpose_z(c - 1, c)
                pe.wait_ge(s_qf, 2 * c + 3)
                keys_values(c + 1, ps_x[0])
                outputs(c, p, 2)
                reciprocals(c, mix)
                outputs(c, p, 3)
                pe.wait_ge(s_qf, 2 * c + 4)
                spread_reciprocals(c)
                state_increments(c + 1)
                key_sums(c + 1, ps_x)
                if mix:
                    mix_k(c - 1, c)
                    mix_r(c - 1, c)
                    mix_v(c - 1)
                else:
                    pe.wait_ge(wo_low, 1)

            def finale(c, p):
                scores(c, p, 0)
                out_projection(c - 1, 0, ps_w)
                out_projection(c - 1, 1, ps_w)
                scores(c, p, 1)
                outputs(c, p, 0)
                denominators(c, ps_x)
                scores(c, p, 2)
                outputs(c, p, 1)
                denominators_by_token(c, ps_x)
                scores(c, p, 3)
                outputs(c, p, 2)
                outputs(c, p, 3)
                reciprocals(c, False, ps_x)
                spread_reciprocals(c)
                transpose_z(c - 1, None)
                pe.wait_ge(s_pr, 8 * c + 8)
                out_projection(c, 0, ps_z)
                out_projection(c, 1, ps_z)
                mix_k(c - 1, None)
                mix_r(c - 1, c)
                mix_v(c - 1)
                transpose_z(c, None, ps_z)
                mix_k(c, None, ps_z)
                mix_r(c, None)
                mix_v(c)

            pe.wait_ge(pool_const, 1)
            pe.wait_ge(kv_in, KV_IN)
            tr(ps_z[0][0:64, 0:64], wc_in[0:64, :], ident[0:64, 0:64])
            for i, w in enumerate((wk_in, wv_in)):
                for k in range(KD):
                    last = tr(ps_z[1][0:64, i * D + k * P:i * D + (k + 1) * P], w[:, k, :], ident[:])
            last.then_inc(prep_ps, 1)
            pe.wait_ge(prep_sb, 1)
            mm(ps_z[0][0:64, 128:128 + KV], wcT[0:64, :], we_in[0:64, :], start=True, stop=True).then_inc(prep_ps, 1)
            transpose_a(0)
            pe.wait_ge(prep_sb, 2)
            pe.wait_ge(bias_lhs, 1)
            for i in range(2):
                for k in range(KD):
                    mm(ps_y[1][:, (k * 2 + i) * KV:(k * 2 + i + 1) * KV], wkvT[0:64, i, k * P:(k + 1) * P],
                       cewe[0:64, :], start=True, stop=True)
            for i in range(2):
                last = mm(ps_y[1][:, 256 + i * KV:256 + (i + 1) * KV], bkv_lhs[0:64, i, :], cewe[0:64, :],
                          start=True, stop=True)
            last.then_inc(prep_ps, 1)
            pe.wait_ge(s_aT, 2)
            pe.wait_ge(prep_sb, 3)
            keys_values(0, ps_w[0])
            pe.wait_ge(wq_ready, 2)
            queries(0, 0)
            queries(0, 1)
            pe.wait_ge(pool_const, 2)
            state_increments(0)
            key_sums(0, (ps_y[0], ps_w[1]))
            pe.wait_ge(ffn_w_in, FFN_IN)
            pe.wait_ge(s_kv, 2)
            pe.wait_ge(s_qf, 2)
            for i, b in enumerate(ffn_banks):
                for k in range(KD):
                    for n in range(KD):
                        last = tr(b[:, (k * KD + n) * P:(k * KD + n + 1) * P], ffn_in[i][:, n, k * P:(k + 1) * P], ident[:])
            last.then_inc(prep_ps, 1)
            pe.wait_ge(rows_in, ROWS_IN)
            pe.wait_ge(dve_const, 2)
            steps(pe, step, finale)

        @block.scalar
        def _(act):
            def copy(dst, src, **kw):
                return nc.scalar.activation(dst, src, ACT.Copy, **kw)

            def a_out(n):
                for k in range(KD):
                    act.wait_ge(s_aT_ps, 2 * n + k + 1)
                    copy(aT[:, k, :], ps_x[k][:, :]).then_inc(s_aT, 1)
                for k in range(KD):
                    act.wait_ge(s_aT, 2 * n + k + 1)
                    copy(aT_p[0][:, k, :], aT[:, k, :]).then_inc(s_aTh, 1)

            def values(n, p):
                for j in range(2):
                    for u in range(2):
                        copy(v_pad[p][HALF * j:HALF * j + HALF, :, u, :, j, :],
                             v_half[HALF * u:HALF * u + HALF, :, 1, :].rearrange("p b (g d) -> p b g d", d=HD)
                             ).then_inc(s_vp, 1)

            def queries_out(n, a):
                act.wait_ge(s_q_ps, 2 * n + a + 1)
                nc.scalar.activation(eq[:, a, :], ps_x[a][:, :], ACT.Relu, bias=neg_bq[:, a:a + 1],
                                     scale=-1.0).then_inc(s_nq, 1)

            def queries_exp(n, a):
                act.wait_ge(s_nq, 2 * n + a + 1)
                nc.scalar.activation(eq[:, a, :], eq[:, a, :], ACT.Exp, scale=-1.0).then_inc(s_eq, 1)

            def keys(n):
                act.wait_ge(s_kv, 2 * n + 1)
                nc.scalar.activation(ek[:], kb[:], ACT.Exp).then_inc(s_ek, 1)
                act.wait_ge(s_kv, 2 * n + 2)
                copy(v_half[0:HALF, :, 0, :], v_half[0:HALF, :, 1, :]).then_inc(s_vh, 1)

            def keys_transposed(n, banks=ps_x):
                act.wait_ge(s_kT_ps, n + 1)
                for j in range(2):
                    copy(kfT[:, :, j, :], banks[0][:, :].rearrange("p (r s) -> p r s", s=HALF), scale=row_mask[:, j:j + 1]).then_inc(s_kT, 1)

            def key_sums(n, banks=ps_x):
                act.wait_ge(s_ks_ps, n + 1)
                if not first(n):
                    act.wait_ge(s_carry, n)
                for b in range(NB):
                    nc.scalar.activation(ksum[:, b * P:(b + 1) * P], banks[1][:, b * P:(b + 1) * P], ACT.Identity,
                                         bias=ksum_carry[:, b:b + 1]).then_inc(s_ks, 1)

            def carry(n):
                act.wait_ge(s_ks, 4 * n + 4)
                copy(ksum_carry[:], ksum[:].rearrange("p (b t) -> p b t", b=NB)[:, :, P - 1]).then_inc(s_carry, 1)

            def denominators(c, banks=ps_w):
                act.wait_ge(s_den_ps, c + 1)
                copy(denT[0:64, :], banks[0][0:64, :]).then_inc(s_denT, 1)

            def reciprocals(c, banks=ps_w):
                act.wait_ge(s_rT_ps, c + 1)
                copy(rdenT[0:32, :], banks[0][0:32, :]).then_inc(s_rT, 1)

            def spread_reciprocals(c):
                for a in range(2):
                    act.wait_ge(s_rb_ps, 2 * c + a + 1)
                    copy(rden_bc[:, a, :], ps_x[a][:, :]).then_inc(s_rb, 1)

            def split_o(c):
                act.wait_ge(s_oT, 2 * c + 2)
                copy(oT_p[0][:], oT[:]).then_inc(s_oTh, 1)

            def split_x(m):
                for k in range(KD):
                    act.wait_ge(s_xk, 2 * m + k + 1)
                    copy(xk_p[0][:, k], xk[:, k]).then_inc(s_xkh, 1)

            def normalise_x(n, p):
                act.wait_ge(x_loaded[p], 8 * n + (16 if p == 0 else 8))
                act.wait_ge(s_rs0, 2 * n + 2)
                act.wait_ge(s_nb0, 2 * n + 2)
                act.wait_ge(s_aT_ps, 2 * n)
                act.wait_ge(s_ab, n)
                for b in range(NB):
                    nc.scalar.activation(a_tok[:, b, :], x_in[p][:, b, :], ACT.Identity, bias=nbias0[:, b:b + 1],
                                         scale=rstd0[:, b:b + 1]).then_inc(s_a, 1)

            def step(c, p, mix):
                a_out(c + 1)
                denominators(c)
                queries_out(c + 1, 0)
                queries_exp(c + 1, 0)
                queries_out(c + 1, 1)
                queries_exp(c + 1, 1)
                if mix:
                    normalise_z(c - 1, 1 - p)
                    shift_z(c - 1)
                keys(c + 1)
                reciprocals(c)
                spread_reciprocals(c)
                if mix:
                    split_x(c - 1)
                keys_transposed(c + 1)
                key_sums(c + 1)
                if mix:
                    channel(c - 1)
                split_o(c)
                carry(c + 1)
                values(c + 1, 1 - p)
                if within(c + 2):
                    normalise_x(c + 2, p)

            def finale(c, p):
                denominators(c, ps_x)
                normalise_z(c - 1, 1 - p)
                reciprocals(c, ps_x)
                spread_reciprocals(c)
                shift_z(c - 1)
                split_o(c)
                split_x(c - 1)
                for k in range(KD):
                    act.wait_ge(s_xr, 2 * c + k - 1)
                    copy(xr_p[0][:, k], xr[:, k]).then_inc(s_xrh, 1)
                channel(c - 1)
                normalise_z(c, p)
                shift_z(c, ps_z)
                split_x(c)
                channel(c, ps_z)

            def normalise_z(m, p):
                act.wait_ge(s_rs2, 2 * m + 2)
                act.wait_ge(s_nb, 2 * m + 2)
                for b in range(NB):
                    nc.scalar.activation(z_tok[:, b, :], x2_tok[p][:, b, :], ACT.Identity, bias=nbias2[:, b:b + 1],
                                         scale=rstd2[:, b:b + 1]).then_inc(s_z, 1)

            def shift_z(m, banks=ps_w):
                copy(zT[:, :, :, 0], zT[:, :, :, P]).then_inc(s_zcar, 1)
                act.wait_ge(s_zcar, m + 1)
                if not first(m):
                    act.wait_ge(s_xr, 2 * m)
                for k in range(KD):
                    act.wait_ge(s_zT_ps, 2 * m + k + 1)
                    copy(zT[:, k, :, 1:P + 1], banks[k][:, :].rearrange("p (b t) -> p b t", b=NB)).then_inc(s_zT, 1)

            def channel(m, banks=ps_w):
                for n in range(2):
                    act.wait_ge(s_k_ps, 2 * m + n + 1)
                    nc.scalar.activation(relu_k[:, n, :], banks[n][:, :], ACT.Relu).then_inc(s_rl, 1)
                    act.wait_ge(s_rl, 2 * m + n + 1)
                    nc.scalar.activation(ka_p[0][:, n, :], relu_k[:, n, :], ACT.Square).then_inc(s_kah, 1)
                    if not first(m) or n:
                        act.wait_ge(s_kal, 2 * m + n)
                    nc.scalar.activation(k_act[:], relu_k[:, n, :], ACT.Square).then_inc(s_ka, 1)
                act.wait_ge(s_out, 2 * m + 1)
                for i in range(2):
                    act.wait_ge(s_r_ps, 2 * m + i + 1)
                    nc.scalar.activation(tanh_r[:, i, :], ps_x[i][:, :], ACT.Tanh, scale=0.5).then_inc(s_th, 1)

            with nc.allow_non_contiguous_dma(reason="bias and mixing vectors, one element a partition"):
                for dst, src in q_loads:
                    act.dma_start(dst, src).then_inc(q_in, 16)
            act.wait_ge(q_in, Q_IN)
            for k in range(KD):
                last = copy(wq_p[0][:, k, :, :].rearrange("p a (g m) -> p a g m", g=G),
                            wq_in[:, k, :].rearrange("p (g a m) -> p a g m", g=G, a=2))
            last.then_inc(wq_ready, 1)
            act.wait_ge(prep_ps, 1)
            copy(wcT[0:64, :], ps_z[0][0:64, 0:64])
            copy(wkvT[0:64, :, :].rearrange("p i n -> p (i n)"), ps_z[1][0:64, :]).then_inc(prep_sb, 1)
            act.wait_ge(prep_ps, 2)
            copy(cewe[0:64, :], ps_z[0][0:64, 128:128 + KV]).then_inc(prep_sb, 1)
            a_out(0)
            act.wait_ge(prep_ps, 3)
            copy(wkv_sb[:].rearrange("p k n -> p (k n)"), ps_y[1][:, 0:256])
            copy(bkv_bc[:], ps_y[1][:, 256:384]).then_inc(prep_sb, 1)
            keys(0)
            act.wait_ge(dve_const, 1)
            queries_out(0, 0)
            queries_out(0, 1)
            queries_exp(0, 0)
            queries_exp(0, 1)
            act.wait_ge(pool_const, 2)
            keys_transposed(0, (ps_y[0], ps_w[1]))
            key_sums(0, (ps_y[0], ps_w[1]))
            carry(0)
            values(0, 0)
            act.wait_ge(prep_ps, 4)
            for w, b in ((wr_p, ffn_banks[0]), (wk_p, ffn_banks[1])):
                copy(w[0][:].rearrange("p k n -> p (k n)"), b[:, :])
            copy(wv_p[0][:].rearrange("p k n -> p (k n)"), ffn_banks[2][:, :], scale=0.5).then_inc(prep_sb, 1)
            act.wait_ge(rows_in, ROWS_IN)
            copy(wo_p[0][:], wo_sb[:]).then_inc(wo_high, 1)
            steps(act, step, finale)

        @block.vector
        def _(dve):
            V = nc.vector
            for t in (*v_pad, v_half, ksum_carry):
                V.memset(t[:], 0.0)
            V.memset(ones64[:], 1.0).then_inc(s_gt, 1)

            def row_stats(src, stats, mv, done, c):
                for b in range(NB):
                    V.bn_stats(stats[:, b, :], src[:, b, :]).then_inc(done, 1)
                dve.wait_ge(done, 8 * c + NB)
                V.memset(wait_carrier[:], 0.0)
                for b in range(NB):
                    V.bn_aggr(mv[:, b, :], stats[:, b, :]).then_inc(done, 1)

            def norm_x(c, p):
                dve.wait_ge(x_loaded[p], 8 * c + (16 if p == 0 else 8))
                if not first(c):
                    dve.wait_ge(s_nb0, 2 * c)
                row_stats(x_in[p], stats0, mv0, s_st0, c)

            def norm_x_scale(c, p):
                dve.wait_ge(s_st0, 8 * c + 8)
                dve.wait_ge(s_rs0, 2 * c + 2)
                if not first(c):
                    dve.wait_ge(s_aT_ps, 2 * c)
                    dve.wait_ge(s_ab, c)
                for b in range(NB):
                    V.tensor_scalar(a_tok[:, b, :], x_in[p][:, b, :], mv0[:, b, 0:1], rstd0[:, b:b + 1], ALU.subtract,
                                    ALU.mult).then_inc(s_a, 1)

            def keys_values(n, p, bank):
                dve.wait_ge(s_kv_ps, n + 1)
                kv = bank[:, :].rearrange("p (b n) -> p b n", b=NB)
                bias = bkv_bc[:].unsqueeze(1).to_broadcast([P, NB, 2 * KV])
                V.tensor_tensor(kb[:], kv[:, :, 0:KV], bias[:, :, 0:KV], ALU.add).then_inc(s_kv, 1)
                V.tensor_tensor(v_half[:, :, 1, :], kv[:, :, KV:2 * KV], bias[:, :, KV:2 * KV], ALU.add).then_inc(s_kv, 1)

            def key_features(n):
                dve.wait_ge(s_ek, n + 1)
                V.tensor_scalar(ek[:], ek[:], 1.0, None, ALU.min).then_inc(s_ekm, 1)
                dve.wait_ge(s_ekm, n + 1)
                for j in range(2):
                    V.scalar_tensor_tensor(out=kf[:, :, j, :], in0=kb[:].rearrange("p b (g d) -> p (b g) d", d=HD),
                                           scalar=1.0, in1=ek[:].rearrange("p b (g d) -> p (b g) d", d=HD),
                                           op0=ALU.add, op1=ALU.max).then_inc(s_kf, 1)

            def queries(n, p, a):
                dve.wait_ge(s_eq, 2 * n + a + 1)
                V.scalar_tensor_tensor(out=qf[p][:, a, :], in0=ps_x[a][:, :], scalar=bq_1[:, a:a + 1],
                                       in1=eq[:, a, :], op0=ALU.add, op1=ALU.max).then_inc(s_qf, 1)

            def add_residual(m, p, i, banks):
                if i == 0:
                    dve.wait_ge(s_ab, m + 1)
                dve.wait_ge(s_y_ps, 2 * m + i + 1)
                V.tensor_tensor(y_tok[:, 2 * i:2 * i + 2, :], banks[i][:, :].rearrange("p (b d) -> p b d", b=2),
                                abo_tok[p][:, 2 * i:2 * i + 2, :], ALU.add).then_inc(s_y, 1)
                if i == 1:
                    dve.wait_ge(s_y, 2 * m + 2)
                    row_stats(y_tok, stats1, mv1, s_st1, m)

            def state_increment(c):
                dve.wait_ge(s_dS_ps, c + 1)
                if not first(c):
                    dve.wait_ge(s_next, c)
                V.tensor_tensor(dstate[:].rearrange("p b u (g j d) -> p (b u g) j d", g=G, j=2),
                                ps_z[1][:, :].rearrange("p (r d) -> p r d", d=HD).unsqueeze(2).to_broadcast([P, 32, 2, HD]),
                                head_rep[:].rearrange("p r (g j d) -> p (r g) j d", g=G, j=2),
                                ALU.mult).then_inc(s_dS, 1)

            def mask(c, b):
                if not (first(c) and b < 2):
                    dve.wait_ge(s_o, 4 * c + b - 1)
                if b == 1 and not first(c):
                    dve.wait_ge(s_oTl, 2 * c)
                for z in range(2):
                    dve.wait_ge(s_sc, 16 * c + 4 * b + z + 3)
                    V.tensor_tensor(probs[:, b % 2, z, :].rearrange("p (r s) -> p r s", s=HALF),
                                    ps_z[z][:, :].rearrange("p (r s) -> p r s", s=HALF),
                                    causal[:].unsqueeze(1).to_broadcast([P, 8, HALF]), ALU.mult).then_inc(s_pr, 1)

            def second_residual(m, p):
                dve.wait_ge(s_st1, 8 * m + 8)
                for b in range(NB):
                    V.scalar_tensor_tensor(out=t_tok[:, b, :], in0=y_tok[:, b, :], scalar=mv1[:, b, 0:1], in1=gamma_bc[:],
                                           op0=ALU.subtract, op1=ALU.mult).then_inc(s_t, 1)
                dve.wait_ge(s_rs1, 2 * m + 2)
                dve.wait_ge(s_xb, m + 1)
                if not first(m):
                    dve.wait_ge(s_out, 2 * m - 1)
                for b in range(NB):
                    dve.wait_ge(s_t, 4 * m + b + 1)
                    V.scalar_tensor_tensor(out=x2_tok[p][:, b, :], in0=t_tok[:, b, :], scalar=rstd1[:, b:b + 1],
                                           in1=xb_tok[p][:, b, :], op0=ALU.mult, op1=ALU.add).then_inc(s_x2, 1)

            def second_stats(m, p):
                dve.wait_ge(s_x2, 4 * m + 4)
                if not first(m):
                    dve.wait_ge(s_nb, 2 * m)
                row_stats(x2_tok[p], stats2, mv2, s_st2, m)

            def reciprocal(c, banks=ps_w):
                dve.wait_ge(s_dtok_ps, c + 1)
                V.tensor_scalar(den[:].rearrange("p b (a n) -> p b a n", a=2),
                                banks[1][:, :].rearrange("p (b a n) -> p b a n", b=NB, a=4)[:, :, 0:2, 0:8],
                                DEN_EPS, None, ALU.add).then_inc(s_den, 1)
                dve.wait_ge(s_den, c + 1)
                V.reciprocal(rden[:], den[:]).then_inc(s_rparts, 1)
                dve.wait_ge(s_rparts, 2 * c + 1)
                V.tensor_copy(rden_parts[:, :, 0, :].bitcast(F32R), rden[:]).then_inc(s_rparts, 1)
                dve.wait_ge(s_rparts, 2 * c + 2)
                V.tensor_tensor(rden_parts[:, :, 1, :], rden[:], rden_parts[:, :, 0, :], ALU.subtract).then_inc(s_rden, 1)

            def middle_state(n, p):
                dve.wait_ge(s_dS, n + 1)
                if not first(n):
                    dve.wait_ge(s_next, n)
                V.tensor_tensor(state[p][:, :, 1, :], state[p][:, :, 0, :], dstate[:, :, 0, :], ALU.add).then_inc(s_mid, 1)

            def divide(c):
                dve.wait_ge(s_o, 4 * c + 4)
                dve.wait_ge(s_rb, 2 * c + 2)
                for u in range(2):
                    V.tensor_tensor(oT[:, :, :, u, :], ps_y[u][:, :].rearrange("p (b a s) -> p a b s", b=NB, a=2),
                                    rden_bc[:].rearrange("p a (b u s) -> p a b u s", b=NB, u=2)[:, :, :, u, :],
                                    ALU.mult).then_inc(s_oT, 1)

            def split_o(c):
                dve.wait_ge(s_oTh, c + 1)
                for a in range(2):
                    V.tensor_tensor(oT_p[1][:, a], oT[:, a], oT_p[0][:, a].bitcast(F32), ALU.subtract).then_inc(s_oTl, 1)

            def token_difference(m):
                for k in range(KD):
                    dve.wait_ge(s_zT, 2 * m + k + 1)
                    V.tensor_tensor(dz[:, k * NB:(k + 1) * NB, :], zT[:, k, :, 1:P + 1], zT[:, k, :, 0:P],
                                    ALU.subtract).then_inc(s_dz, 1)

            def token_shift(m, dst, mu, done):
                for k in range(KD):
                    dve.wait_ge(s_dz, 2 * m + k + 1)
                    V.scalar_tensor_tensor(out=dst[:, k], in0=dz[:, k * NB:(k + 1) * NB, :], scalar=mu[:, k:k + 1],
                                           in1=zT[:, k, :, 0:P], op0=ALU.mult, op1=ALU.add).then_inc(done, 1)

            def split_r(m):
                for k in range(KD):
                    dve.wait_ge(s_xr, 2 * m + k + 1)
                    V.tensor_copy(xr_p[0][:, k], xr[:, k]).then_inc(s_xrh, 1)
                low_part(m, xr, xr_p, s_xrh, s_xrl)

            def split_k(m):
                low_part(m, xk, xk_p, s_xkh, s_xkl)

            def low_part(m, x, x_p, high_done, done):
                for k in range(KD):
                    dve.wait_ge(high_done, 2 * m + k + 1)
                    V.tensor_tensor(x_p[1][:, k], x[:, k], x_p[0][:, k].bitcast(F32), ALU.subtract).then_inc(done, 1)

            for_k, for_r = (xk, mu_k_col, s_xk), (xr, mu_r_col, s_xr)

            def square_k(m):
                for i in range(2):
                    dve.wait_ge(s_ka, 2 * m + i + 1)
                    dve.wait_ge(s_kah, 2 * m + i + 1)
                    V.tensor_tensor(ka_p[1][:, i], k_act[:], ka_p[0][:, i].bitcast(F32), ALU.subtract).then_inc(s_kal, 1)

            def gate(m):
                dve.wait_ge(s_out, 2 * m + 1)
                for i in range(2):
                    gate_half(m, i)

            def gate_half(m, i):
                dve.wait_ge(s_th, 2 * m + i + 1)
                dve.wait_ge(s_v_ps, 2 * m + i + 1)
                V.scalar_tensor_tensor(out=gated[:, i, :], in0=tanh_r[:, i, :], scalar=1.0, in1=ps_w[i][:, :],
                                       op0=ALU.add, op1=ALU.mult).then_inc(s_gt, 1)

            def mix_weights():
                dve.wait_ge(prep_sb, 4)
                for w, b in ((wr_p, ffn_banks[0]), (wk_p, ffn_banks[1])):
                    V.tensor_tensor(w[1][:].rearrange("p k n -> p (k n)"), b[:, :],
                                    w[0][:].bitcast(F32).rearrange("p k n -> p (k n)"), ALU.subtract).then_inc(weights_low, 1)
                V.scalar_tensor_tensor(out=wv_p[1][:].rearrange("p k n -> p (k n)"), in0=ffn_banks[2][:, :], scalar=0.5,
                                       in1=wv_p[0][:].bitcast(F32).rearrange("p k n -> p (k n)"), op0=ALU.mult,
                                       op1=ALU.subtract).then_inc(weights_low, 1)

            def step(c, p, mix):
                mask(c, 0)
                if not mix:
                    mix_weights()
                if mix:
                    add_residual(c - 1, 1 - p, 0, ps_w)
                    add_residual(c - 1, 1 - p, 1, ps_w)
                mask(c, 1)
                if mix:
                    second_residual(c - 1, 1 - p)
                    second_stats(c - 1, 1 - p)
                mask(c, 2)
                queries(c + 1, 1 - p, 0)
                reciprocal(c)
                queries(c + 1, 1 - p, 1)
                mask(c, 3)
                keys_values(c + 1, 1 - p, ps_x[0])
                key_features(c + 1)
                if mix:
                    token_shift(c - 1, *for_k)
                    split_k(c - 1)
                    token_shift(c - 1, *for_r)
                    split_r(c - 1)
                    square_k(c - 1)
                if mix:
                    divide(c)
                state_increment(c + 1)
                middle_state(c + 1, 1 - p)
                if not mix:
                    divide(c)
                    split_o(c)
                if mix:
                    gate(c - 1)
                if within(c + 2):
                    norm_x(c + 2, p)

            def finale(c, p):
                mask(c, 0)
                add_residual(c - 1, 1 - p, 0, ps_w)
                add_residual(c - 1, 1 - p, 1, ps_w)
                mask(c, 1)
                second_residual(c - 1, 1 - p)
                mask(c, 2)
                reciprocal(c, ps_x)
                second_stats(c - 1, 1 - p)
                mask(c, 3)
                divide(c)
                split_o(c)
                token_shift(c - 1, *for_k)
                split_k(c - 1)
                token_shift(c - 1, *for_r)
                dve.wait_ge(s_xkl, 2 * c)
                add_residual(c, p, 0, ps_z)
                add_residual(c, p, 1, ps_z)
                dve.wait_ge(s_xr, 2 * c)
                second_residual(c, p)
                second_stats(c, p)
                gate(c - 1)
                token_difference(c)
                token_shift(c, *for_k)
                split_k(c)
                token_shift(c, *for_r)
                split_r(c)
                square_k(c)
                dve.wait_ge(s_out, 2 * c + 1)
                for i in range(2):
                    gate_half(c, i)
                    dve.wait_ge(out_stored, 16 * c + 16)
                    dve.wait_ge(s_gt, 2 * c + i + 2)
                    V.tensor_tensor(out_tok[:, 2 * i:2 * i + 2, :], gated[:, i].rearrange("p (b d) -> p b d", b=2),
                                    x2_tok[p][:, 2 * i:2 * i + 2, :], ALU.add).then_inc(s_out, 1)

            norm_x(0, 0)
            dve.wait_ge(pool_const, 1)
            for j in range(2):
                V.tensor_reduce(row_mask[:, j:j + 1], head_ones[:, j:8:2], AX_X, ALU.add)
            dve.wait_ge(q_in, Q_IN)
            V.tensor_scalar(neg_bq[:], bq_col[:], -1.0, None, ALU.mult)
            V.tensor_scalar(bq_1[:], bq_col[:], 1.0, None, ALU.add).then_inc(dve_const, 1)
            dve.wait_ge(dve_const, 1)
            norm_x_scale(0, 0)
            dve.wait_ge(kv_in, KV_IN)
            for i in range(2):
                last = V.tensor_scalar(bkv_lhs[0:64, i, :], ones64[0:64, :], bkv_col[0:64, i:i + 1], None, ALU.mult)
            last.then_inc(bias_lhs, 1)
            norm_x(1, 1)
            dve.wait_ge(wq_ready, 1)
            for k in range(KD):
                last = V.tensor_tensor(wq_p[1][:, k, :, :].rearrange("p a (g m) -> p a g m", g=G),
                                       wq_in[:, k, :].rearrange("p (g a m) -> p a g m", g=G, a=2),
                                       wq_p[0][:, k, :, :].bitcast(F32).rearrange("p a (g m) -> p a g m", g=G), ALU.subtract)
            last.then_inc(wq_ready, 1)
            dve.wait_ge(s_aTh, 2)
            V.tensor_tensor(aT_p[1][:], aT[:], aT_p[0][:].bitcast(F32), ALU.subtract).then_inc(s_aTl, 1)
            dve.wait_ge(prep_sb, 3)
            keys_values(0, 0, ps_w[0])
            key_features(0)
            queries(0, 0, 0)
            queries(0, 0, 1)
            dve.wait_ge(pool_const, 2)
            V.tensor_copy(spread_r[0:32], spread[0:32]).then_inc(dve_const, 1)
            state_increment(0)
            middle_state(0, 0)
            norm_x_scale(1, 1)
            dve.wait_ge(rows_in, ROWS_IN)
            steps(dve, step, finale)


_INS = ['L0_attn_x', 'L0_attn_Wq', 'L0_attn_bq', 'L0_attn_Wk', 'L0_attn_bk', 'L0_attn_Wv', 'L0_attn_bv', 'L0_attn_Wc',
        'L0_attn_We', 'L0_attn_Wo', 'L0_attn_bo', 'L0_attn_gamma', 'L0_attn_beta', 'L0_ffn_W_r', 'L0_ffn_W_k',
        'L0_ffn_W_v', 'L0_ffn_mu_r', 'L0_ffn_mu_k']


def kernel(**inputs):
    import numpy as _np
    import concourse.bacc as _bacc
    from concourse import mybir as _mybir
    from concourse.bass_utils import run_bass_kernel_spmd as _run

    nc = _bacc.Bacc("TRN2", target_bir_lowering=False, num_devices=1)
    arrays, args = {}, []
    for name in _INS:
        a = _np.ascontiguousarray(inputs[name])
        arrays[f"in_{name}_dram"] = a
        args.append(nc.dram_tensor(f"in_{name}_dram", a.shape, _mybir.dt.from_np(a.dtype), kind="ExternalInput").ap())
    args.append(nc.dram_tensor("out_dram", inputs['L0_attn_x'].shape, _mybir.dt.float32, kind="ExternalOutput").ap())
    build(nc, *args)
    r = _run(nc, [arrays], core_ids=[0])
    return r.results[0]["out_dram"]
```
